# Optimizing a Trainium2 kernel written in Bass

```python
import numpy as np
import jax
import jax.numpy as jnp

def _softmax(x, axis=-1):
    return jax.nn.softmax(x, axis=axis)

def _gelu(x):
    return jax.nn.gelu(x, approximate=True)

def _silu(x):
    return jax.nn.silu(x)

def _sigmoid(x):
    return jax.nn.sigmoid(x)

def _layernorm(x, axis=-1, eps=1e-05):
    m = jnp.mean(x, axis=axis, keepdims=True)
    v = jnp.var(x, axis=axis, keepdims=True)
    return (x - m) / jnp.sqrt(v + eps)

def _scatter_add(tgt, idx, src, axis=0):
    return tgt.at[idx].add(src)

def _segment_sum(src, seg, n):
    return jax.ops.segment_sum(src, seg, n)
kernel_name = 'mk_adaln_ffn_d1_seqx_r8_3f3190'

def setup_inputs(seed: int=0):
    np.random.seed(seed)
    _w = jnp.asarray

    def _rec_inputs():
        import jax
        import jax.numpy as jnp
        _rk = jax.random.key(seed)
        x = 7.22e-05 + 1 * jax.random.normal(jax.random.fold_in(_rk, 1), (8, 256, 128), jnp.float32)
        _lenS = 256 - jax.random.randint(jax.random.fold_in(_rk, 7), (8,), 0, max(1, 256 // 4) + 1, jnp.int32)
        _lenS2 = 256 - jax.random.randint(jax.random.fold_in(_rk, 8), (8,), 0, max(1, 256 // 4) + 1, jnp.int32)
        cond_8 = -0.104238 + 1.01173 * jax.random.normal(jax.random.fold_in(_rk, 11), (8, 8), jnp.float32)
        return (x, cond_8)
    x, cond_8 = _rec_inputs()

    def _L0_cond_setup():
        import jax, jax.numpy as jnp
        import numpy as np
        TOP_K = 2
        NUM_MOE_LAYERS = 12

        def _gemma_mlp(x, gate_w, up_w, down_w):
            g = jnp.einsum('bsh,hi->bsi', x, gate_w)
            u = jnp.einsum('bsh,hi->bsi', x, up_w)
            return jnp.einsum('bsi,ih->bsh', jax.nn.gelu(g, approximate=True) * u, down_w)
        key = jax.random.key(seed)
        ks = jax.random.split(key, 8)
        B, S, H, I, E = (32, 32, 128, 512, 8)
        std = 0.02
        return {'x': jax.random.normal(ks[0], (B, S, H), jnp.float32), 'router_logits': jax.random.normal(ks[1], (B, E), jnp.float32), 'skill_gate': jax.random.normal(ks[2], (E, H, I), jnp.float32) * std, 'skill_up': jax.random.normal(ks[3], (E, H, I), jnp.float32) * std, 'skill_down': jax.random.normal(ks[4], (E, I, H), jnp.float32) * std, 'shared_gate': jax.random.normal(ks[5], (H, I), jnp.float32) * std, 'shared_up': jax.random.normal(ks[6], (H, I), jnp.float32) * std, 'shared_down': jax.random.normal(ks[7], (I, H), jnp.float32) * std}
    _L0_cond_all = _L0_cond_setup()
    _L0_cond_in = {k: v for k, v in _L0_cond_all.items() if k in ('skill_gate', 'skill_up', 'skill_down', 'shared_gate', 'shared_up', 'shared_down')}
    del _L0_cond_all

    def _L0_ffn_setup():
        import jax, jax.numpy as jnp
        import numpy as np
        D_MODEL = 128
        EXPERT_DIM = 256
        N_EXPERTS = 8
        LN_EPS = 1e-05

        def _bit_quant(W):
            scale = jnp.clip(jnp.mean(jnp.abs(W), axis=-1, keepdims=True), 1e-05, None)
            w_q = jnp.clip(jnp.round(W / scale), -1.0, 1.0) * scale
            return W + jax.lax.stop_gradient(w_q - W)
        key = jax.random.key(seed)
        ks = jax.random.split(key, 7)
        x = jax.random.normal(ks[0], (4, 256, D_MODEL), dtype=jnp.float32)
        shared_w1 = jax.random.normal(ks[1], (EXPERT_DIM, D_MODEL), dtype=jnp.float32) / np.sqrt(EXPERT_DIM)
        shared_w2 = jax.random.normal(ks[2], (D_MODEL, EXPERT_DIM), dtype=jnp.float32) / np.sqrt(D_MODEL)
        expert_w1 = jax.random.normal(ks[3], (N_EXPERTS, EXPERT_DIM, D_MODEL), dtype=jnp.float32) / np.sqrt(EXPERT_DIM)
        expert_w2 = jax.random.normal(ks[4], (N_EXPERTS, D_MODEL, EXPERT_DIM), dtype=jnp.float32) / np.sqrt(D_MODEL)
        router_w = 0.02 * jax.random.normal(ks[5], (N_EXPERTS, D_MODEL), dtype=jnp.float32)
        ln_gamma = jnp.ones((D_MODEL,), dtype=jnp.float32)
        ln_beta = jnp.zeros((D_MODEL,), dtype=jnp.float32)
        return {'x': x, 'shared_w1': shared_w1, 'shared_w2': shared_w2, 'expert_w1': expert_w1, 'expert_w2': expert_w2, 'router_w': router_w, 'ln_gamma': ln_gamma, 'ln_beta': ln_beta}
    _L0_ffn_all = _L0_ffn_setup()
    _L0_ffn_in = {k: v for k, v in _L0_ffn_all.items() if k in ('shared_w1', 'shared_w2', 'expert_w1', 'expert_w2', 'router_w', 'ln_gamma', 'ln_beta')}
    del _L0_ffn_all
    return {'x': x, 'cond_8': cond_8, 'L0_cond_skill_gate': _L0_cond_in['skill_gate'], 'L0_cond_skill_up': _L0_cond_in['skill_up'], 'L0_cond_skill_down': _L0_cond_in['skill_down'], 'L0_cond_shared_gate': _L0_cond_in['shared_gate'], 'L0_cond_shared_up': _L0_cond_in['shared_up'], 'L0_cond_shared_down': _L0_cond_in['shared_down'], 'L0_ffn_shared_w1': _L0_ffn_in['shared_w1'], 'L0_ffn_shared_w2': _L0_ffn_in['shared_w2'], 'L0_ffn_expert_w1': _L0_ffn_in['expert_w1'], 'L0_ffn_expert_w2': _L0_ffn_in['expert_w2'], 'L0_ffn_router_w': _L0_ffn_in['router_w'], 'L0_ffn_ln_gamma': _L0_ffn_in['ln_gamma'], 'L0_ffn_ln_beta': _L0_ffn_in['ln_beta']}

def reference(x, cond_8, L0_cond_skill_gate, L0_cond_skill_up, L0_cond_skill_down, L0_cond_shared_gate, L0_cond_shared_up, L0_cond_shared_down, L0_ffn_shared_w1, L0_ffn_shared_w2, L0_ffn_expert_w1, L0_ffn_expert_w2, L0_ffn_router_w, L0_ffn_ln_gamma, L0_ffn_ln_beta):
    import jax
    import jax.numpy as jnp

    def _L0_cond_ref(x, router_logits, skill_gate, skill_up, skill_down, shared_gate, shared_up, shared_down):
        import jax, jax.numpy as jnp
        import numpy as np
        TOP_K = 2
        NUM_MOE_LAYERS = 12

        def _gemma_mlp(x, gate_w, up_w, down_w):
            g = jnp.einsum('bsh,hi->bsi', x, gate_w)
            u = jnp.einsum('bsh,hi->bsi', x, up_w)
            return jnp.einsum('bsi,ih->bsh', jax.nn.gelu(g, approximate=True) * u, down_w)
        B = x.shape[0]
        E = skill_gate.shape[0]
        rw = jax.nn.softmax(router_logits.astype(jnp.float32), axis=-1)
        w, sel = jax.lax.top_k(rw, TOP_K)
        w = w / w.sum(axis=-1, keepdims=True)
        w = w.astype(x.dtype)
        scale = 1.0 / NUM_MOE_LAYERS
        w = scale * w + (1.0 - scale) * jax.lax.stop_gradient(w)
        dense_w = jnp.zeros((B, E), x.dtype).at[jnp.arange(B)[:, None], sel].add(w)

        def step(acc, params):
            g, u, d, we = params
            return (acc + we[:, None, None] * _gemma_mlp(x, g, u, d), None)
        out, _ = jax.lax.scan(step, jnp.zeros_like(x), (skill_gate, skill_up, skill_down, dense_w.T))
        out = out + _gemma_mlp(x, shared_gate, shared_up, shared_down)
        return out

    def _L0_ffn_ref(x, shared_w1, shared_w2, expert_w1, expert_w2, router_w, ln_gamma, ln_beta):
        import jax, jax.numpy as jnp
        import numpy as np
        D_MODEL = 128
        EXPERT_DIM = 256
        N_EXPERTS = 8
        LN_EPS = 1e-05

        def _bit_quant(W):
            scale = jnp.clip(jnp.mean(jnp.abs(W), axis=-1, keepdims=True), 1e-05, None)
            w_q = jnp.clip(jnp.round(W / scale), -1.0, 1.0) * scale
            return W + jax.lax.stop_gradient(w_q - W)
        mu = jnp.mean(x, axis=-1, keepdims=True)
        var = jnp.mean(jnp.square(x - mu), axis=-1, keepdims=True)
        h = (x - mu) / jnp.sqrt(var + LN_EPS) * ln_gamma + ln_beta
        sw1, sw2 = (_bit_quant(shared_w1), _bit_quant(shared_w2))
        shared_out = jax.nn.silu(jnp.einsum('btd,fd->btf', h, sw1)) @ sw2.T
        probs = jax.nn.softmax(h @ router_w.T, axis=-1)
        top_prob = jnp.max(probs, axis=-1)
        top_idx = jnp.argmax(probs, axis=-1)
        ew1, ew2 = (_bit_quant(expert_w1), _bit_quant(expert_w2))
        h1 = jax.nn.silu(jnp.einsum('btd,efd->ebtf', h, ew1))
        eo = jnp.einsum('ebtf,edf->ebtd', h1, ew2)
        gate = jax.nn.one_hot(top_idx, N_EXPERTS, dtype=h.dtype) * top_prob[..., None]
        routed_out = jnp.einsum('ebtd,bte->btd', eo, gate)
        return shared_out + routed_out
    x = x + _L0_ffn_ref(_L0_cond_ref(x, cond_8, L0_cond_skill_gate, L0_cond_skill_up, L0_cond_skill_down, L0_cond_shared_gate, L0_cond_shared_up, L0_cond_shared_down), L0_ffn_shared_w1, L0_ffn_shared_w2, L0_ffn_expert_w1, L0_ffn_expert_w2, L0_ffn_router_w, L0_ffn_ln_gamma, L0_ffn_ln_beta)
    return x

_drawn_inputs = setup_inputs


def setup_inputs(seed=0):
    import zlib

    import numpy as np

    out = dict(_drawn_inputs(seed))
    spreads = {'L0_ffn_ln_gamma': (1.0, 0.2), 'L0_ffn_ln_beta': (0.0, 0.291)}
    factors = {}
    for name, (base, spread) in spreads.items():
        noise = np.random.default_rng([zlib.crc32(name.encode()), seed]).standard_normal(out[name].shape)
        drawn = base * np.exp(spread * noise) if base else spread * noise
        out[name] = jnp.asarray(drawn.astype(out[name].dtype))
    for name, factor in factors.items():
        out[name] = (out[name] * factor).astype(out[name].dtype)
    return out
```

```python
from contextlib import ExitStack

import concourse.bass as bass
from concourse import mybir


P = 128
ALU = mybir.AluOpType
ACT = mybir.ActivationFunctionType
F32 = mybir.dt.float32
F16 = mybir.dt.float16
U32 = mybir.dt.uint32
AX = mybir.AxisListType.X

WS = 256.0
LN_EPS = 1e-5
MIN_SCALE = 1e-5


def span(start, size):
    return slice(start, start + size) if isinstance(start, int) else bass.ds(start, size)


def moe_adaln_ffn(nc, x, cond, g_w, u_w, d_w, sg_w, su_w, sd_w, fs1, fs2, fe1, fe2, router, gamma, beta, out):
    B, S, D = x.shape
    E, _, I = g_w.shape
    NE, F, _ = fe1.shape
    assert (B, S, D, E, I, NE, F) == (8, 256, P, 8, 512, 8, 256)
    T = B * S
    BT = 2 * S
    NB = T // BT
    NT = BT // P
    NJ = S // P
    W = 3 * I
    SH = E
    NF = NE + 1
    FC = F // P
    TW = 2 * F
    K2 = 2
    CH = FC * NF
    DOWN_LAG = 3
    GROUPS = NB + 1
    Y_LAG = 4

    mask_dram = nc.dram_tensor("mask_scratch", (NB, NE * BT), F16, kind="Internal").ap()

    with ExitStack() as ctx:
        def sb(name, shape, dt=F32):
            return ctx.enter_context(nc.sbuf_tensor(name, shape, dt))

        def sem(name):
            return ctx.enter_context(nc.semaphore(name))

        ident = sb("ident", [P, P])
        ident16 = sb("ident16", [P, P], F16)
        rank_desc = sb("rank_desc", [P, NT, NE])
        neg_half = sb("neg_half", [P, NT])
        cond_sb = sb("cond_sb", [P, B, E])
        router_sb = sb("router_sb", [NE, P])
        routerT = sb("routerT", [P, NE])
        gamma_sb = sb("gamma_sb", [P, 1])
        beta_sb = sb("beta_sb", [P, 1])
        top_v = sb("top_v", [P, B, 8])
        top_i = sb("top_i", [P, B * 8], U32)
        top_d = sb("top_d", [P, B])
        top_e = sb("top_e", [P, B])
        top_s = sb("top_s", [P, B])
        mix_w = sb("mix_w", [P, B * K2])
        x_tok = sb("x_tok", [P, T])
        x16 = sb("x16", [P, 2, T], F16)
        region = sb("region", [P, NB * NE * BT // 2])
        raw = region[:, 0:3 * W].rearrange("p (s w) -> p s w", s=3)
        mask_sb = region[:, :].bitcast(F16)
        w16 = sb("w16", [P, (E + 1) * 2 * W], F16)
        f1_raw = sb("f1_raw", [P, NF * F])
        f2_raw = sb("f2_raw", [P, NF * F])
        sum1 = sb("sum1", [P, NF * FC])
        sum2 = sb("sum2", [P, NF])
        sc1 = sb("sc1", [P, NF * FC])
        sc2 = sb("sc2", [P, NF])
        hs1 = sb("hs1", [P, 2, NF * FC])
        hs2 = sb("hs2", [P, 2, NF])
        abs_junk = sb("abs_junk", [P, 2 * TW], F16)
        above = sb("above", [P, TW], F16)
        below = sb("below", [P, TW], F16)
        tern = sb("tern", [P, NF * TW], F16)
        ternT = sb("ternT", [P, NF * TW], F16)
        sc2T = sb("sc2T", [NE, P])
        g_sb = sb("g_sb", [P, 2, 2 * S])
        a_sb = sb("a_sb", [P, 2, 2 * S])
        a16 = sb("a16", [P, 4, 2, 2 * S], F16)
        shared = sb("shared", [P, T])
        c_sb = sb("c_sb", [P, BT])
        stats = sb("stats", [P, NT, 6])
        msum, mdif, mdif2, m2, mean = (sb(n, [P, NT]) for n in ("msum", "mdif", "mdif2", "m2", "mean"))
        var_e = sb("var_e", [P, NT])
        rstd = sb("rstd", [P, NT])
        norm = sb("norm", [P, NT, P])
        h_sb = sb("h_sb", [P, BT])
        h16 = sb("h16", [P, 2, T], F16)
        lmax = sb("lmax", [P, NT])
        ldif = sb("ldif", [P, NT, NE])
        lth = sb("lth", [P, NT, NE])
        lden = sb("lden", [P, NT, NE])
        lex = sb("lex", [P, NT, NE])
        score = sb("score", [P, NT, NE])
        smax = sb("smax", [P, NT])
        lsum = sb("lsum", [P, NT])
        prob = sb("prob", [P, NT])
        route = sb("route", [P, NT, P])
        maskT = sb("maskT", [NE, T], F16)
        gateT = sb("gateT", [NE, T])
        w16_old = w16[:, :].rearrange("p (e h w) -> p e h w", e=E + 1, h=2)
        s16 = w16_old[:, 0:6, :, 0:BT]
        hm = w16_old[:, 0:3, :, BT:2 * BT]
        s_sb = [w16_old[:, 6 + r, 0, 0:2 * BT].bitcast(F32) for r in range(3)]
        y_shared, y_gate = g_sb[:, 0, :], g_sb[:, 1, :]
        y_sum, out_sb = a_sb[:, 0, :], a_sb[:, 1, :]

        def bank(name):
            return ctx.enter_context(nc.psum_tensor(name, [P, 512], F32))

        ps_gate = [bank("ps_gate0"), bank("ps_gate1")]
        ps_up = [bank("ps_up0"), bank("ps_up1")]
        ps_out = [bank("ps_out0"), bank("ps_out1")]
        ps_a = bank("ps_a")
        ps_b = bank("ps_b")
        ps_b16 = ps_b[:, :].bitcast(F16)
        z_bank = [ps_gate[0], ps_up[0], ps_gate[1]]
        ps_ys, ps_yr = ps_up[1], ps_out[0]

        x_in = [sem(f"x_in{n}") for n in range(NB)]
        shared_in = [sem(f"shared_in{n}") for n in range(3)]
        expert_in = [sem("expert_in_even"), sem("expert_in_odd")]
        cond_in = sem("cond_in")
        small_in = sem("small_in")
        ffn_in = sem("ffn_in")
        const_done = sem("const_done")
        const_step = sem("const_step")
        xt_done = sem("xt_done")
        xhi_done = sem("xhi_done")
        xlo_done = sem("xlo_done")
        whi_done = sem("whi_done")
        wlo_done = sem("wlo_done")
        rt_ready = sem("rt_ready")
        rt_copied = sem("rt_copied")
        pick = sem("pick")
        pick_exp = sem("pick_exp")
        gu_done = sem("gu_done")
        gelu_done = sem("gelu_done")
        prod_done = sem("prod_done")
        ahi_done = sem("ahi_done")
        alo_done = sem("alo_done")
        down_done = sem("down_done")
        out_taken = sem("out_taken")
        t1_done = sem("t1_done")
        st_step = sem("st_step")
        var_done = sem("var_done")
        rstd_done = sem("rstd_done")
        norm_done = sem("norm_done")
        t2_done = sem("t2_done")
        h_done = sem("h_done")
        hhi_done = sem("hhi_done")
        hlo_done = sem("hlo_done")
        logits_done = sem("logits_done")
        rstep = sem("rstep")
        ldif_done = sem("ldif_done")
        tanh_done = sem("tanh_done")
        route_done = sem("route_done")
        routeT_done = sem("routeT_done")
        maskT_done = sem("maskT_done")
        gateT_done = sem("gateT_done")
        mask_out = sem("mask_out")
        mask_in = sem("mask_in")
        abs_done = sem("abs_done")
        sc_step = sem("sc_step")
        thr_done = sem("thr_done")
        tstep = sem("tstep")
        tern_done = sem("tern_done")
        ternT_done = sem("ternT_done")
        ternT_copied = sem("ternT_copied")
        hm_done = sem("hm_done")
        z_done = sem("z_done")
        silu_done = sem("silu_done")
        shi_act = sem("shi_act")
        shi_dve = sem("shi_dve")
        slo_done = sem("slo_done")
        y_done = sem("y_done")
        ys_taken = sem("ys_taken")
        yg_done = sem("yg_done")
        yg_copied = sem("yg_copied")
        yr_taken = sem("yr_taken")
        ysum_done = sem("ysum_done")
        yT_done = sem("yT_done")
        out_ready = sem("out_ready")
        out_stored = sem("out_stored")


        ONE_AHEAD = dict(pe=[logits_done, routeT_done, yT_done], act=[gateT_done, yg_copied],
                         dve=[out_taken, hlo_done, route_done, ysum_done, out_ready])

        block = ctx.enter_context(nc.Block())

        def w_cols(e, part, col):
            return span(e * (2 * W) + (part * W + col), P)

        def w_hi(e, col, size):
            return span(e * (2 * W) + col, size)

        def w_lo(e, col, size):
            return span(e * (2 * W) + (W + col), size)

        def spread(ap, n):
            return ap.unsqueeze(2).broadcast_to([P, ap.shape[1], n])

        def act_hi(c):
            return c % 3 != 2

        def act_hi_count(c):
            return sum(act_hi(m) for m in range(c + 1))

        ACT_HIS, DVE_HIS = act_hi_count(CH - 1), CH - act_hi_count(CH - 1)

        @block.sync
        def _(sp):
            sp.sem_inc(out_stored, 16)
            for n in range(NB):
                sp.dma_start(x_tok[:, n * BT:(n + 1) * BT].rearrange("p (b r) -> p b r", b=2),
                             x[2 * n:2 * n + 2].rearrange("b (p j) d -> p b (j d)", j=NJ)).then_inc(x_in[n], 16)

            def load_expert(e, slot):
                sp.dma_start(raw[:, slot, 0:I], g_w[e]).then_inc(expert_in[slot], 16)
                sp.dma_start(raw[:, slot, I:2 * I], u_w[e]).then_inc(expert_in[slot], 16)
                sp.dma_start(raw[:, slot, 2 * I:W].rearrange("p (c d) -> p c d", d=D),
                             d_w[e].rearrange("(c p) d -> p c d", p=P)).then_inc(expert_in[slot], 16)

            load_expert(0, 0)
            load_expert(1, 1)
            sp.dma_start(f1_raw[:, 0:F].rearrange("p (c d) -> p c d", d=D),
                         fs1.rearrange("(c p) d -> p c d", p=P)).then_inc(ffn_in, 16)
            sp.dma_start(f1_raw[:, F:].rearrange("p (c d) -> p c d", d=D),
                         fe1.rearrange("e (c p) d -> p (e c) d", p=P)).then_inc(ffn_in, 16)
            sp.dma_start(f2_raw[:, 0:F], fs2).then_inc(ffn_in, 16)
            sp.dma_start(f2_raw[:, F:].rearrange("p (e f) -> p e f", f=F),
                         fe2.rearrange("e d f -> d e f")).then_inc(ffn_in, 16)
            for e in range(2, E):
                sp.wait_ge(wlo_done, e)
                load_expert(e, e % 2)
            sp.wait_ge(wlo_done, E + 1)
            for n in range(NB):
                sp.wait_ge(maskT_done, n + 1)
                sp.dma_start(mask_dram[n].rearrange("(e t) -> e t", e=NE),
                             maskT[:, n * BT:(n + 1) * BT]).then_inc(mask_out, 16)
                sp.wait_ge(mask_out, 16 * (n + 1))
                sp.dma_start(mask_sb[:, n * NE * BT:(n + 1) * NE * BT],
                             mask_dram[n].partition_broadcast(P)).then_inc(mask_in, 16)
                sp.wait_ge(mask_in, 16 * (n + 1))
            for n in range(NB):
                sp.wait_ge(out_ready, n + 2)
                sp.dma_start(out[2 * n:2 * n + 2].rearrange("b (p j) d -> p b (j d)", j=NJ),
                             out_sb.rearrange("p (b r) -> p b r", b=2)).then_inc(out_stored, 16)
            sp.wait_ge(out_stored, 16 * NB + 16)

        @block.tensor
        def _(pe):
            for ahead in ONE_AHEAD["pe"]:
                pe.sem_inc(ahead, 1)
            def gate_up(q, e, batch):
                half, xs = q % 2, span(batch * S, S)
                for bank_, base in ((ps_gate[half], 0), (ps_up[half], I)):
                    for m in range(2):
                        col = base + (2 * half + m) * P
                        dst = bank_[:, m * S:(m + 1) * S]
                        pe.matmul(dst, w16[:, w_cols(e, 0, col)], x16[:, 0, xs], start=True, stop=False)
                        pe.matmul(dst, w16[:, w_cols(e, 0, col)], x16[:, 1, xs], start=False, stop=False)
                        last = pe.matmul(dst, w16[:, w_cols(e, 1, col)], x16[:, 0, xs], start=False, stop=True)
                last.then_inc(gu_done, 1)

            def down(d, e, dst, first, final):
                for m in range(2):
                    col = 2 * I + (2 * (d % 2) + m) * P
                    hi, lo = (a16[:, d % 4, part, m * S:(m + 1) * S] for part in range(2))
                    pe.matmul(dst, w16[:, w_cols(e, 0, col)], hi, start=first and m == 0, stop=False)
                    pe.matmul(dst, w16[:, w_cols(e, 0, col)], lo, start=False, stop=False)
                    last = pe.matmul(dst, w16[:, w_cols(e, 1, col)], hi, start=False, stop=final and m == 1)
                last.then_inc(down_done, 1)

            x_bank = [ps_out[0], ps_out[1], ps_a, ps_b]
            pe.wait_ge(const_done, 1)
            for n in range(NB):
                pe.wait_ge(x_in[n], 16)
                for t in range(NT):
                    last = pe.transpose(x_bank[n][:, t * P:(t + 1) * P], x_tok[:, (n * NT + t) * P:(n * NT + t + 1) * P], ident[:, :])
                last.then_inc(xt_done, 1)
            pe.wait_ge(small_in, 48)
            pe.transpose(ps_up[1][:, 0:NE], router_sb[:, :], ident[0:NE, 0:NE]).then_inc(rt_ready, 1)

            def shared_turn(i, first):
                for q in range(4):
                    if q == 0:
                        pe.wait_ge(xlo_done, i + 1)
                    if first and q == 0:
                        pe.wait_ge(wlo_done, 1)
                    if first and q == 1:
                        pe.wait_ge(rt_copied, 1)
                    if not first or q >= 2:
                        pe.wait_ge(prod_done, i * 4 + (q - 1))
                    gate_up(q, SH, i * 2 + q // 2)
                    d = q - DOWN_LAG
                    if first and d < 0:
                        continue
                    pe.wait_ge(alo_done, i * 4 + (d + 1))
                    if d % 2 == 0:
                        if first:
                            pe.wait_ge(xlo_done, 2)
                        else:
                            pe.wait_ge(out_taken, i * 2 + d // 2)
                    down(d, SH, ps_out[(d % 4) // 2][:, 0:S], d % 2 == 0, d % 2 == 1)

            shared_turn(0, True)
            with pe.Fori(1, B // 2) as i:
                shared_turn(i, False)

            def tern_transpose(group):
                for k, f in enumerate(group):
                    for m in range(TW // P):
                        last = pe.transpose(ps_b16[:, k * TW + m * P:k * TW + (m + 1) * P],
                                            tern[:, span(f * TW + m * P, P)], ident16[:, :])
                last.then_inc(ternT_done, 1)

            def to_tokens(n):
                pe.wait_ge(out_taken, n * 2 + (B + 3))
                for t in range(NT):
                    last = pe.transpose(ps_a[:, t * P:(t + 1) * P], c_sb[:, t * P:(t + 1) * P], ident[:, :])
                last.then_inc(t1_done, 1)

            def to_features(n):
                pe.wait_ge(norm_done, n + 1)
                for t in range(NT):
                    last = pe.transpose(ps_a[:, t * P:(t + 1) * P], norm[:, t, :], ident[:, :])
                last.then_inc(t2_done, 1)

            def logits(n, groups_copied):
                pe.wait_ge(ternT_copied, groups_copied)
                pe.wait_ge(h_done, n + 1)
                for t in range(NT):
                    last = pe.matmul(ps_b[:, t * NE:(t + 1) * NE], h_sb[:, t * P:(t + 1) * P], routerT[:, :],
                                     start=True, stop=True)
                last.then_inc(logits_done, 1)

            def route_transpose(n):
                pe.wait_ge(route_done, n + 2)
                for t in range(NT):
                    last = pe.transpose(ps_b[:, t * P:(t + 1) * P], route[:, t, :], ident[:, :])
                last.then_inc(routeT_done, 1)

            def chosen_turn(i, first=False, norming=True, routing=True):
                def chosen(turn, unit):
                    at = top_i[0:1, span(turn * 16 + (unit // 2 * 8 + unit % 2), 1)]
                    return pe.value_load(at, min_val=0, max_val=E - 1)

                here = [chosen(i, unit) for unit in range(4)]
                before = [SH, SH] if first else [chosen(i - 1, 2), chosen(i - 1, 3)]
                for q in range(8):
                    pe.wait_ge(prod_done, i * 8 + (2 * B + q - 1))
                    gate_up(q, here[q // 2], i * 2 + q // 4)
                    if q == 0 and norming:
                        if routing:
                            pe.wait_ge(gateT_done, i - 1)
                        pe.wait_ge(tern_done, i)
                        tern_transpose([i * 2 - 2, i * 2 - 1])
                    if q == 1 and routing:
                        to_features(i - 2)
                    if q == 3 and routing:
                        logits(i - 2, i)
                    if q == 5 and norming:
                        to_tokens(i - 1)
                    if q == 6 and routing:
                        route_transpose(i - 2)
                    d = q - DOWN_LAG
                    pe.wait_ge(alo_done, i * 8 + (2 * B + d + 1))
                    if first and d < 0:
                        if d % 2 == 0:
                            pe.wait_ge(out_taken, B + d // 2)
                        down(d, SH, ps_out[(d % 4) // 2][:, 0:S], d % 2 == 0, d % 2 == 1)
                    else:
                        if d % 4 == 0:
                            pe.wait_ge(out_taken, i * 2 + (B + d // 4))
                        e = here[d // 2] if d >= 0 else before[(d % 4) // 2]
                        down(d, e, ps_out[(d % 8) // 4][:, 0:S], d % 4 == 0, d % 4 == 3)

            pe.wait_ge(pick, 2 * B)
            pe.wait_ge(wlo_done, E + 1)
            chosen_turn(0, first=True, norming=False, routing=False)
            chosen_turn(1, routing=False)
            with pe.Fori(2, NB) as i:
                chosen_turn(i)
            at = top_i[0:1, (B - 1) * 8 + 1:(B - 1) * 8 + 2]
            last_e = pe.value_load(at, min_val=0, max_val=E - 1)
            at = top_i[0:1, (B - 1) * 8:(B - 1) * 8 + 1]
            last_e0 = pe.value_load(at, min_val=0, max_val=E - 1)

            def first_layer(k, c):
                f = c // FC
                w = ternT[:, f * TW + (c % FC) * P:f * TW + (c % FC + 1) * P]
                for part in range(2):
                    rhs = h16[:, part, span(k * BT, BT)] if f == 0 else hm[:, f % 3, part, :]
                    last = pe.matmul(z_bank[c % 3][:, :], w, rhs, start=part == 0, stop=part == 1)
                last.then_inc(z_done, 1)

            def second_layer(c):
                f = c // FC
                w = ternT[:, f * TW + F + (c % FC) * P:f * TW + F + (c % FC + 1) * P]
                dst = ps_ys if f == 0 else ps_yr
                for part in range(2):
                    last = pe.matmul(dst[:, :], w, s16[:, c % 6, part, :], start=c in (0, FC) and part == 0,
                                     stop=c in (FC - 1, CH - 1) and part == 1)
                last.then_inc(y_done, 1)

            def gate_product(n):
                pe.wait_ge(gateT_done, n + 2)
                pe.wait_ge(ternT_copied, GROUPS + 1)
                pe.matmul(ps_out[1][:, :], sc2T[:, :], gateT[:, span(n * BT, BT)],
                          start=True, stop=True).then_inc(yg_done, 1)

            def y_transpose(n):
                pe.wait_ge(ysum_done, n + 2)
                for t in range(NT):
                    last = pe.transpose(ps_a[:, t * P:(t + 1) * P], y_sum[:, t * P:(t + 1) * P], ident[:, :])
                last.then_inc(yT_done, 1)

            def second_layer_turn(k, c, first):
                m = c - Y_LAG
                pe.wait_ge(slo_done, k * CH + (m + 1))
                if m == 0:
                    if first:
                        pe.wait_ge(prod_done, 4 * B + 2 * B)
                    else:
                        pe.wait_ge(ys_taken, k)
                if m == FC:
                    if first:
                        pe.wait_ge(out_taken, 2 * B)
                    else:
                        pe.wait_ge(yr_taken, k)
                second_layer(m % CH)

            def ffn_turn(k, first):
                for c in range(CH):
                    f = c // FC
                    if not first or c >= 3:
                        pe.wait_ge(silu_done, k * CH + (c - 2))
                    elif c != 1:
                        pe.wait_ge(prod_done, 4 * B + 2 * B - (c == 0))
                    if first and c % FC == 0:
                        pe.wait_ge(ternT_copied, f // 2 + 1)
                    if c == 0:
                        pe.wait_ge(hlo_done, k + 2)
                    elif c % FC == 0:
                        pe.wait_ge(hm_done, k * NE + f)
                    first_layer(k, c)
                    if first and c < 3:
                        d = c + 5
                        pe.wait_ge(alo_done, 4 * B + 2 * B - 3 + c + 1)
                        down(d, (last_e0 if d == 5 else last_e), ps_out[1][:, 0:S], False, d == 7)
                    if not first and c == 0:
                        pe.wait_ge(out_taken, 2 * B + 1)
                        pe.wait_ge(yg_copied, k)
                        gate_product(k - 1)
                    if not first and c == 8:
                        pe.wait_ge(out_ready, k)
                        y_transpose(k - 1)
                    if first:
                        if c == 0:
                            pe.wait_ge(gateT_done, 3)
                            pe.wait_ge(tern_done, 4)
                            tern_transpose([6, 7])
                        if c == 1:
                            to_features(2)
                        if c == 3:
                            logits(2, 4)
                        if c == 5:
                            to_tokens(3)
                        if c == 7:
                            route_transpose(2)
                        if c == 9:
                            pe.wait_ge(gateT_done, 4)
                            pe.wait_ge(tern_done, 5)
                            pe.wait_ge(thr_done, GROUPS)
                            pe.transpose(ps_b[0:NE, 2 * P:3 * P], sc2[:, 1:NF], ident[:, :])
                            tern_transpose([8])
                        if c == 10:
                            to_features(3)
                        if c == 12:
                            logits(3, 5)
                        if c == 16:
                            route_transpose(3)
                    if not first or c >= Y_LAG:
                        second_layer_turn(k, c, first)

            ffn_turn(0, True)
            with pe.Fori(1, NB) as k:
                ffn_turn(k, False)
            pe.wait_ge(yg_copied, NB)
            gate_product(NB - 1)
            for c in range(Y_LAG):
                second_layer_turn(NB, c, False)
            pe.wait_ge(out_ready, NB)
            y_transpose(NB - 1)

        @block.scalar
        def _(act):
            for ahead in ONE_AHEAD["act"]:
                act.sem_inc(ahead, 1)
            act.dma_start(cond_sb[:, :, :].rearrange("p b e -> p (b e)"),
                          cond.rearrange("b e -> (b e)").partition_broadcast(P)).then_inc(cond_in, 16)
            act.dma_start(raw[:, 2, 0:I], sg_w).then_inc(shared_in[0], 16)
            act.dma_start(raw[:, 2, I:2 * I], su_w).then_inc(shared_in[1], 16)
            act.dma_start(raw[:, 2, 2 * I:W].rearrange("p (c d) -> p c d", d=D),
                          sd_w.rearrange("(c p) d -> p c d", p=P)).then_inc(shared_in[2], 16)
            act.dma_start(router_sb[:, :], router).then_inc(small_in, 16)
            act.dma_start(gamma_sb[:, :], gamma.rearrange("(p a) -> p a", a=1)).then_inc(small_in, 16)
            act.dma_start(beta_sb[:, :], beta.rearrange("(p a) -> p a", a=1)).then_inc(small_in, 16)

            act.wait_ge(pick, 2 * B + 1)
            act.activation(top_e[:, :], top_d[:, :], ACT.Exp).then_inc(pick_exp, 1)

            x_bank = [ps_out[0], ps_out[1], ps_a, ps_b]
            for part in range(3):
                act.wait_ge(shared_in[part], 16)
                act.activation(w16[:, w_hi(SH, part * I, I)], raw[:, 2, part * I:(part + 1) * I], ACT.Copy,
                               scale=WS).then_inc(whi_done, 1)
                if part == 0:
                    for n in range(NB):
                        act.wait_ge(xt_done, n + 1)
                        act.activation(x16[:, 0, n * BT:(n + 1) * BT], x_bank[n][:, :],
                                       ACT.Copy).then_inc(xhi_done, 1)
            act.wait_ge(rt_ready, 1)
            act.activation(routerT[:, :], ps_up[1][:, 0:NE], ACT.Copy).then_inc(rt_copied, 1)

            def gelu(q):
                act.activation(g_sb[:, q % 2, :], ps_gate[q % 2][:, :], ACT.Gelu_apprx_tanh,
                               scale=1.0 / WS).then_inc(gelu_done, 1)

            def act_part_hi(q):
                act.activation(a16[:, q % 4, 0, :], a_sb[:, q % 2, :], ACT.Copy).then_inc(ahi_done, 1)

            def expert_hi(slot, e, loads):
                act.wait_ge(expert_in[slot], loads)
                act.activation(w16[:, w_hi(e, 0, W)], raw[:, slot, :], ACT.Copy, scale=WS).then_inc(whi_done, 1)

            def shared_turn(i, first):
                for q in range(4):
                    act.wait_ge(gu_done, i * 4 + (q + 1))
                    if not first or q >= 2:
                        act.wait_ge(prod_done, i * 4 + (q - 1))
                    gelu(q)
                    if not first or q >= 1:
                        act.wait_ge(prod_done, i * 4 + q)
                        if not first:
                            act.wait_ge(down_done, i * 4 + (q - 3))
                        act_part_hi(q - 1)
                    if q % 2 == 1:
                        expert_hi(q // 2, i * 2 + q // 2, i * 48 + 48)

            shared_turn(0, True)
            with act.Fori(1, B // 2) as i:
                shared_turn(i, False)

            def abs_sums(g, group):
                act.wait_ge(thr_done, g)
                for k, f in enumerate(group):
                    junk = abs_junk[:, k * TW:(k + 1) * TW]
                    for c in range(FC):
                        act.activation(junk[:, c * P:(c + 1) * P], f1_raw[:, span(f * (FC * P) + c * P, P)], ACT.Abs,
                                       accum_out=sum1[:, span(f * FC + c, 1)])
                    last = act.activation(junk[:, F:TW], f2_raw[:, span(f * F, F)], ACT.Abs,
                                          accum_out=sum2[:, span(f, 1)])
                last.then_inc(abs_done, 1)

            def copy_ternT(g, group):
                act.wait_ge(ternT_done, g + 1)
                act.activation(ternT[:, span(group[0] * TW, len(group) * TW)], ps_b16[:, 0:len(group) * TW],
                               ACT.Copy).then_inc(ternT_copied, 1)

            def features(n):
                act.wait_ge(t2_done, n + 1)
                act.wait_ge(logits_done, n + 1)
                act.wait_ge(hlo_done, n + 1)
                act.activation(h_sb[:, :], ps_a[:, :], ACT.Identity, bias=beta_sb[:, :],
                               scale=gamma_sb[:, :]).then_inc(h_done, 1)
                act.wait_ge(h_done, n + 1)
                act.activation(h16[:, 0, span(n * BT, BT)], h_sb[:, :], ACT.Copy).then_inc(hhi_done, 1)

            def half_tanh(n):
                act.wait_ge(ldif_done, n + 1)
                act.wait_ge(route_done, n + 1)
                act.activation(lth[:, :, :], ldif[:, :, :], ACT.Tanh, scale=0.5).then_inc(tanh_done, 1)

            def copy_route(n):
                act.wait_ge(routeT_done, n + 2)
                act.activation(maskT[:, span(n * BT, BT)], ps_b[0:NE, :], ACT.Copy).then_inc(maskT_done, 1)
                act.activation(gateT[:, span(n * BT, BT)], ps_b[32:32 + NE, :], ACT.Copy).then_inc(gateT_done, 1)

            def chosen_turn(i, norming=True, routing=True):
                for q in range(8):
                    act.wait_ge(gu_done, i * 8 + (2 * B + q + 1))
                    act.wait_ge(prod_done, i * 8 + (2 * B + q - 1))
                    gelu(q)
                    act.wait_ge(prod_done, i * 8 + (2 * B + q))
                    act.wait_ge(down_done, i * 8 + (2 * B + q - 4))
                    act_part_hi(q - 1)
                    if q == 1 and norming:
                        copy_ternT(i - 1, [i * 2 - 2, i * 2 - 1])
                    if q == 2 and routing:
                        features(i - 2)
                    if q == 3:
                        abs_sums(i, [i * 2, i * 2 + 1])
                    if q == 4 and routing:
                        half_tanh(i - 2)
                    if q == 7 and routing:
                        copy_route(i - 2)

            act.wait_ge(small_in, 48)
            act.wait_ge(ffn_in, 64)
            chosen_turn(0, norming=False, routing=False)
            chosen_turn(1, routing=False)
            with act.Fori(2, NB) as i:
                chosen_turn(i)

            def chunk_hi(k, c, m, early):
                if act_hi(m % CH):
                    act.wait_ge(silu_done, k * CH + (m + 1))
                    if not early:
                        act.wait_ge(y_done, k * CH + (m - 5))
                    act.activation(s16[:, m % 6, 0, :], s_sb[m % 3], ACT.Copy).then_inc(shi_act, 1)

            def ffn_turn(k, first):
                for c in range(CH):
                    act.wait_ge(z_done, k * CH + (c + 1))
                    if not first or c >= 3:
                        act.wait_ge(slo_done, k * CH + (c - 2))
                    f = c // FC
                    act.activation(s_sb[c % 3], z_bank[c % 3][:, :], ACT.Silu,
                                   scale=sc1[:, f * FC + c % FC:f * FC + c % FC + 1]).then_inc(silu_done, 1)
                    if not first or c >= 1:
                        chunk_hi(k, c, c - 1, first and c < 7)
                    if not first and c == 1:
                        act.wait_ge(yg_done, k)
                        act.wait_ge(ysum_done, k)
                        act.activation(y_gate, ps_out[1][:, :], ACT.Copy).then_inc(yg_copied, 1)
                    if c == 7:
                        act.wait_ge(y_done, k * CH + FC)
                        act.wait_ge(ysum_done, k + 1)
                        act.activation(y_shared, ps_ys[:, :], ACT.Copy,
                                       scale=sc2[:, 0:1]).then_inc(ys_taken, 1)
                    if first:
                        if c == 1:
                            copy_ternT(3, [6, 7])
                        if c == 3:
                            features(2)
                        if c == 5:
                            half_tanh(2)
                        if c == 8:
                            copy_route(2)
                        if c == 10:
                            copy_ternT(4, [8])
                            act.activation(sc2T[:, :], ps_b[0:NE, 2 * P:3 * P], ACT.Copy).then_inc(ternT_copied, 1)
                        if c == 11:
                            features(3)
                        if c == 14:
                            half_tanh(3)
                        if c == 17:
                            copy_route(3)

            act.wait_ge(prod_done, 6 * B)
            act.wait_ge(down_done, 6 * B - 4)
            act_part_hi(7)
            abs_sums(4, [8])
            act.wait_ge(thr_done, 4)
            ffn_turn(0, True)
            with act.Fori(1, NB) as k:
                ffn_turn(k, False)
            chunk_hi(NB, 0, -1, False)
            act.wait_ge(yg_done, NB)
            act.wait_ge(ysum_done, NB)
            act.activation(y_gate, ps_out[1][:, :], ACT.Copy).then_inc(yg_copied, 1)

        @block.vector
        def _(dve):
            for ahead in ONE_AHEAD["dve"]:
                dve.sem_inc(ahead, 1)
            mix = mix_w[:, :].rearrange("p (b k) -> p b k", k=K2)
            dve.wait_ge(cond_in, 16)
            for b in range(B):
                dve.max(top_v[:, b, :], cond_sb[:, b, :]).then_inc(pick, 1)
                dve.wait_ge(pick, 2 * b + 1)
                dve.max_index(top_i[:, b * 8:(b + 1) * 8], top_v[:, b, :], cond_sb[:, b, :]).then_inc(pick, 1)
            dve.tensor_tensor(top_d[:, :], top_v[:, :, 1], top_v[:, :, 0], ALU.subtract).then_inc(pick, 1)
            dve.wait_ge(pick_exp, 1)
            dve.tensor_scalar(top_s[:, :], top_e[:, :], 1.0, None, ALU.add).then_inc(pick, 1)
            dve.wait_ge(pick, 2 * B + 2)
            dve.reciprocal(mix[:, :, 0], top_s[:, :]).then_inc(pick, 1)
            dve.wait_ge(pick, 2 * B + 3)
            dve.tensor_tensor(mix[:, :, 1], mix[:, :, 0], top_e[:, :], ALU.mult).then_inc(pick, 1)

            x_bank = [ps_out[0], ps_out[1], ps_a, ps_b]

            def weight_lo(e, slot, col, size):
                return dve.scalar_tensor_tensor(out=w16[:, w_lo(e, col, size)], in0=raw[:, slot, col:col + size],
                                                scalar=WS, in1=w16[:, w_hi(e, col, size)],
                                                op0=ALU.mult, op1=ALU.subtract)

            for part in range(3):
                dve.wait_ge(whi_done, part + 1)
                last = weight_lo(SH, 2, part * I, I)
                if part == 0:
                    for n in range(NB):
                        dve.wait_ge(xhi_done, n + 1)
                        dve.tensor_tensor(x16[:, 1, n * BT:(n + 1) * BT], x_bank[n][:, :],
                                          x16[:, 0, n * BT:(n + 1) * BT], ALU.subtract).then_inc(xlo_done, 1)
            last.then_inc(wlo_done, 1)

            def product(q, weight):
                dve.scalar_tensor_tensor(out=a_sb[:, q % 2, :], in0=g_sb[:, q % 2, :], scalar=weight,
                                         in1=ps_up[q % 2][:, :], op0=ALU.mult, op1=ALU.mult).then_inc(prod_done, 1)

            def act_part_lo(q):
                dve.tensor_tensor(a16[:, q % 4, 1, :], a_sb[:, q % 2, :], a16[:, q % 4, 0, :],
                                  ALU.subtract).then_inc(alo_done, 1)

            def take_shared(u, half, cols_at):
                dve.wait_ge(down_done, u * 2 + 2)
                dve.tensor_scalar(shared[:, span(cols_at, S)], ps_out[half][:, 0:S], 1.0 / (WS * WS), None,
                                  ALU.mult).then_inc(out_taken, 1)

            def shared_turn(i, first):
                for q in range(4):
                    dve.wait_ge(gelu_done, i * 4 + (q + 1))
                    if not first or q >= 2:
                        dve.wait_ge(alo_done, i * 4 + (q - 1))
                    product(q, 1.0)
                    if q % 2 == 1:
                        if not first:
                            take_shared(i * 2 + (q // 2 - 2), q // 2, i * (2 * S) + (q // 2 - 2) * S)
                        e = i * 2 + q // 2
                        dve.wait_ge(whi_done, e + 4)
                        weight_lo(e, q // 2, 0, W).then_inc(wlo_done, 1)

            shared_turn(0, True)
            with dve.Fori(1, B // 2) as i:
                shared_turn(i, False)

            def take_batch(n, b):
                dve.wait_ge(down_done, n * 8 + (2 * B + 4 * b + 4))
                if b == 0:
                    dve.wait_ge(t1_done, n)
                dve.scalar_tensor_tensor(out=c_sb[:, b * S:(b + 1) * S], in0=ps_out[b][:, 0:S],
                                         scalar=1.0 / (WS * WS), in1=shared[:, span(n * BT + b * S, S)],
                                         op0=ALU.mult, op1=ALU.add).then_inc(out_taken, 1)

            def statistics(n):
                dve.wait_ge(t1_done, n + 1)
                for t in range(NT):
                    last = dve.bn_stats(stats[:, t, :], ps_a[:, t * P:(t + 1) * P])
                last.then_inc(st_step, 1)
                dve.wait_ge(st_step, n * 3 + 1)
                dve.tensor_tensor(msum[:, :], stats[:, :, 1], stats[:, :, 4], ALU.add)
                dve.tensor_tensor(mdif[:, :], stats[:, :, 1], stats[:, :, 4], ALU.subtract)
                dve.tensor_tensor(m2[:, :], stats[:, :, 2], stats[:, :, 5], ALU.add).then_inc(st_step, 1)
                dve.wait_ge(st_step, n * 3 + 2)
                dve.tensor_scalar(mean[:, :], msum[:, :], 0.5, None, ALU.mult)
                dve.scalar_tensor_tensor(out=mdif2[:, :], in0=mdif[:, :], scalar=0.25, in1=mdif[:, :],
                                         op0=ALU.mult, op1=ALU.mult)
                dve.tensor_scalar(m2[:, :], m2[:, :], 1.0 / D, LN_EPS, ALU.mult, ALU.add).then_inc(st_step, 1)
                dve.wait_ge(st_step, n * 3 + 3)
                dve.wait_ge(rstd_done, n)
                dve.tensor_tensor(var_e[:, :], m2[:, :], mdif2[:, :], ALU.add).then_inc(var_done, 1)

            def normalise(n):
                dve.wait_ge(rstd_done, n + 1)
                dve.wait_ge(t2_done, n)
                for t in range(NT):
                    last = dve.tensor_scalar(norm[:, t, :], ps_a[:, t * P:(t + 1) * P], mean[:, t:t + 1],
                                             rstd[:, t:t + 1], ALU.subtract, ALU.mult)
                last.then_inc(norm_done, 1)

            def h_lo(n):
                dve.wait_ge(hhi_done, n + 1)
                dve.tensor_tensor(h16[:, 1, span(n * BT, BT)], h_sb[:, :], h16[:, 0, span(n * BT, BT)],
                                  ALU.subtract).then_inc(hlo_done, 1)

            RS = 9

            def choose(n):
                lg = ps_b[:, 0:NT * NE].rearrange("p (t e) -> p t e", e=NE)
                dve.wait_ge(logits_done, n + 2)
                dve.tensor_reduce(lmax[:, :], lg, AX, ALU.max).then_inc(rstep, 1)
                dve.wait_ge(rstep, n * RS + 1)
                dve.tensor_tensor(ldif[:, :, :], lg, spread(lmax[:, :], NE), ALU.subtract).then_inc(ldif_done, 1)
                dve.wait_ge(ldif_done, n + 1)
                dve.scalar_tensor_tensor(out=score[:, :, :], in0=ldif[:, :, :], scalar=0.0, in1=rank_desc[:, :, :],
                                         op0=ALU.is_ge, op1=ALU.mult).then_inc(rstep, 1)
                dve.wait_ge(rstep, n * RS + 2)
                dve.tensor_reduce(smax[:, :], score[:, :, :], AX, ALU.max).then_inc(rstep, 1)
                dve.wait_ge(rstep, n * RS + 3)
                dve.wait_ge(routeT_done, n + 1)
                dve.tensor_tensor(route[:, :, 0:NE], score[:, :, :], spread(smax[:, :], NE),
                                  ALU.is_equal).then_inc(rstep, 1)

            def gates(n):
                dve.wait_ge(tanh_done, n + 1)
                dve.tensor_scalar(lden[:, :, :], lth[:, :, :], -1.0, 1.0, ALU.mult, ALU.add).then_inc(rstep, 1)
                dve.wait_ge(rstep, n * RS + 5)
                dve.reciprocal(lden[:, :, :], lden[:, :, :]).then_inc(rstep, 1)
                dve.wait_ge(rstep, n * RS + 6)
                dve.scalar_tensor_tensor(out=lex[:, :, :], in0=lth[:, :, :], scalar=1.0, in1=lden[:, :, :],
                                         op0=ALU.add, op1=ALU.mult).then_inc(rstep, 1)
                dve.wait_ge(rstep, n * RS + 7)
                dve.tensor_reduce(lsum[:, :], lex[:, :, :], AX, ALU.add).then_inc(rstep, 1)
                dve.wait_ge(rstep, n * RS + 8)
                dve.reciprocal(prob[:, :], lsum[:, :]).then_inc(rstep, 1)
                dve.wait_ge(rstep, n * RS + 9)
                dve.tensor_tensor(route[:, :, 32:32 + NE], route[:, :, 0:NE], spread(prob[:, :], NE),
                                  ALU.mult).then_inc(route_done, 1)

            def thresholds(g, f, size):
                one, two = span(f * FC, size * FC), span(f, size)
                dve.wait_ge(abs_done, g + 1)
                dve.tensor_scalar(sc1[:, one], sum1[:, one], 1.0 / D, MIN_SCALE, ALU.mult, ALU.max)
                dve.tensor_scalar(sc2[:, two], sum2[:, two], 1.0 / F, MIN_SCALE, ALU.mult,
                                  ALU.max).then_inc(sc_step, 1)
                dve.wait_ge(sc_step, g + 1)
                for sign in range(2):
                    dve.tensor_scalar(hs1[:, sign, one], sc1[:, one], 0.5 - sign, None, ALU.mult)
                    last = dve.tensor_scalar(hs2[:, sign, two], sc2[:, two], 0.5 - sign, None, ALU.mult)
                last.then_inc(thr_done, 1)

            def chosen_turn(i, first=False, norming=True, routing=True):
                for q in range(8):
                    dve.wait_ge(gelu_done, i * 8 + (2 * B + q + 1))
                    dve.wait_ge(alo_done, i * 8 + (2 * B + q - 1))
                    product(q, mix_w[:, span(i * 4 + (q // 4 * 2 + q // 2 % 2), 1)])
                    if not first or q >= 1:
                        dve.wait_ge(ahi_done, i * 8 + (2 * B + q))
                        dve.wait_ge(down_done, i * 8 + (2 * B + q - 4))
                        act_part_lo(q - 1)
                    if first and q in (1, 3):
                        take_shared(B - 2 + q // 2, q // 2, (B - 2 + q // 2) * S)
                    if q == 2 and routing:
                        h_lo(i - 2)
                    if q == 3 and norming:
                        take_batch(i - 1, 1)
                    if q == 4:
                        thresholds(i, i * 2, 2)
                        if routing:
                            choose(i - 2)
                    if q == 5 and norming:
                        statistics(i - 1)
                    if q == 5 and routing:
                        gates(i - 2)
                    if q == 7:
                        take_batch(i, 0)
                        if norming:
                            normalise(i - 1)

            dve.wait_ge(pick, 2 * B + 4)
            dve.wait_ge(const_done, 1)
            chosen_turn(0, first=True, norming=False, routing=False)
            chosen_turn(1, routing=False)
            with dve.Fori(2, NB) as i:
                chosen_turn(i)

            def mask_tokens(k, f):
                mask = mask_sb[:, span(k * (NE * BT) + (f - 1) * BT, BT)].unsqueeze(1).broadcast_to([P, 2, BT])
                dve.tensor_tensor(hm[:, f % 3, :, :], h16[:, :, span(k * BT, BT)], mask,
                                  ALU.mult).then_inc(hm_done, 1)

            def chunk_parts(k, m, early):
                his = act_hi_count(m)
                if not early:
                    dve.wait_ge(y_done, k * CH + (m - 5))
                if act_hi(m % CH):
                    dve.wait_ge(shi_act, k * ACT_HIS + his)
                else:
                    dve.wait_ge(silu_done, k * CH + (m + 1))
                    dve.tensor_copy(s16[:, m % 6, 0, :], s_sb[m % 3]).then_inc(shi_dve, 1)
                    dve.wait_ge(shi_dve, k * DVE_HIS + (m + 1 - his))
                dve.tensor_tensor(s16[:, m % 6, 1, :], s_sb[m % 3], s16[:, m % 6, 0, :],
                                  ALU.subtract).then_inc(slo_done, 1)

            def add_y(n):
                dve.wait_ge(y_done, n * CH + CH)
                dve.wait_ge(yg_copied, n + 2)
                dve.tensor_tensor(y_gate, ps_yr[:, :], y_gate, ALU.mult).then_inc(yr_taken, 1)
                dve.wait_ge(yr_taken, n + 1)
                dve.wait_ge(ys_taken, n + 1)
                dve.wait_ge(yT_done, n + 1)
                dve.tensor_tensor(y_sum, y_gate, y_shared, ALU.add).then_inc(ysum_done, 1)

            def finish(n):
                dve.wait_ge(yT_done, n + 2)
                dve.wait_ge(out_stored, n * 16 + 16)
                dve.tensor_tensor(out_sb, ps_a[:, :], x_tok[:, span(n * BT, BT)],
                                  ALU.add).then_inc(out_ready, 1)

            def ffn_turn(k, first):
                dve.wait_ge(mask_in, k * 16 + 16)
                for c in range(CH):
                    f = c + 1 if c < 2 else c // 2 + 2
                    if f <= NE and (c < 2 or c % 2 == 0):
                        if f > 3:
                            dve.wait_ge(z_done, k * CH + (f - 2) * FC)
                        elif not first:
                            dve.wait_ge(z_done, k * CH)
                        mask_tokens(k, f)
                    if first and c == 0:
                        dve.wait_ge(ahi_done, 6 * B)
                        dve.wait_ge(down_done, 6 * B - 4)
                        act_part_lo(7)
                    if not first or c >= 1:
                        chunk_parts(k, c - 1, first and c < 7)
                    if not first and c == 4:
                        add_y(k - 1)
                    if not first and c == 10:
                        finish(k - 1)
                    if first:
                        if c == 1:
                            thresholds(4, 8, 1)
                        if c == 3:
                            h_lo(2)
                            take_batch(3, 1)
                        if c == 4:
                            choose(2)
                        if c == 6:
                            gates(2)
                            statistics(3)
                        if c == 8:
                            normalise(3)
                        if c == 11:
                            h_lo(3)
                        if c == 13:
                            choose(3)
                        if c == 15:
                            gates(3)

            ffn_turn(0, True)
            with dve.Fori(1, NB) as k:
                ffn_turn(k, False)
            chunk_parts(NB, -1, False)
            add_y(NB - 1)
            finish(NB - 1)

        @block.gpsimd
        def _(pool):
            pool.memset(ident[:, :], 0.0).then_inc(const_step, 1)
            pool.wait_ge(const_step, 1)
            pool.affine_select(out=ident[:, :], in_=ident[:, :], compare_op=ALU.not_equal, fill=1.0, base=0,
                               pattern=[[-1, P]], channel_multiplier=1).then_inc(const_step, 1)
            pool.wait_ge(const_step, 2)
            pool.tensor_copy(ident16[:, :], ident[:, :])
            for e in range(NE):
                pool.memset(rank_desc[:, :, e], float(NE - e))
            pool.memset(neg_half[:, :], -0.5).then_inc(const_step, 1)
            pool.memset(route[:, :, :], 0.0).then_inc(const_done, 1)

            def shared_turn(i, first):
                for q in range(4):
                    pool.wait_ge(ahi_done, i * 4 + (q + 1))
                    if not first:
                        pool.wait_ge(down_done, i * 4 + (q - 3))
                    pool.tensor_tensor(a16[:, q, 1, :], a_sb[:, q % 2, :], a16[:, q, 0, :],
                                       ALU.subtract).then_inc(alo_done, 1)

            shared_turn(0, True)
            with pool.Fori(1, B // 2) as i:
                shared_turn(i, False)

            def round_weights(g, f, last_of_group):
                pool.wait_ge(thr_done, g + 1)
                for sign, (dst, op) in enumerate(((above, ALU.is_gt), (below, ALU.is_lt))):
                    for c in range(FC):
                        n = f * FC + c
                        pool.tensor_scalar(dst[:, c * P:(c + 1) * P], f1_raw[:, n * P:(n + 1) * P],
                                           hs1[:, sign, n:n + 1], None, op)
                    last = pool.tensor_scalar(dst[:, F:TW], f2_raw[:, f * F:(f + 1) * F], hs2[:, sign, f:f + 1],
                                              None, op)
                last.then_inc(tstep, 1)
                pool.wait_ge(tstep, 2 * f + 1)
                done = pool.tensor_tensor(tern[:, f * TW:(f + 1) * TW], above[:, :], below[:, :], ALU.subtract)
                done.then_inc(tstep, 1)
                pool.wait_ge(tstep, 2 * f + 2)
                if last_of_group:
                    pool.sem_inc(tern_done, 1)

            def inverse_deviation(n):
                pool.wait_ge(const_step, 3)
                pool.wait_ge(var_done, n + 1)
                pool.wait_ge(norm_done, n)
                pool.tensor_tensor(rstd[:, :], var_e[:, :], neg_half[:, :], ALU.pow).then_inc(rstd_done, 1)

            for g in range(NB):
                round_weights(g, 2 * g, False)
                if g >= 1:
                    inverse_deviation(g - 1)
                round_weights(g, 2 * g + 1, True)
            round_weights(NB, 2 * NB, True)
            inverse_deviation(NB - 1)


_INS = ["x", "cond_8", "L0_cond_skill_gate", "L0_cond_skill_up", "L0_cond_skill_down", "L0_cond_shared_gate",
        "L0_cond_shared_up", "L0_cond_shared_down", "L0_ffn_shared_w1", "L0_ffn_shared_w2", "L0_ffn_expert_w1",
        "L0_ffn_expert_w2", "L0_ffn_router_w", "L0_ffn_ln_gamma", "L0_ffn_ln_beta"]


def kernel(**inputs):
    import numpy as np
    import concourse.bacc as bacc
    from concourse.bass_utils import run_bass_kernel_spmd

    nc = bacc.Bacc("TRN2", target_bir_lowering=False, num_devices=1)
    arrays, args = {}, []
    for name in _INS:
        a = np.ascontiguousarray(inputs[name])
        arrays[f"in_{name}"] = a
        args.append(nc.dram_tensor(f"in_{name}", a.shape, mybir.dt.from_np(a.dtype), kind="ExternalInput").ap())
    out = nc.dram_tensor("out", arrays["in_x"].shape, F32, kind="ExternalOutput").ap()
    moe_adaln_ffn(nc, *args, out)
    r = run_bass_kernel_spmd(nc, [arrays], core_ids=[0])
    return r.results[0]["out"]
```

```python
from contextlib import ExitStack

import concourse.bass as bass
from concourse import mybir


P = 128
ALU = mybir.AluOpType
ACT = mybir.ActivationFunctionType
F32 = mybir.dt.float32
F16 = mybir.dt.float16
U32 = mybir.dt.uint32
AX = mybir.AxisListType.X

WS = 256.0
LN_EPS = 1e-5
MIN_SCALE = 1e-5


def span(start, size):
    return slice(start, start + size) if isinstance(start, int) else bass.ds(start, size)


def moe_adaln_ffn(nc, x, cond, g_w, u_w, d_w, sg_w, su_w, sd_w, fs1, fs2, fe1, fe2, router, gamma, beta, out):
    B, S, D = x.shape
    E, _, I = g_w.shape
    NE, F, _ = fe1.shape
    assert (B, S, D, E, I, NE, F) == (8, 256, P, 8, 512, 8, 256)
    T = B * S
    BT = 2 * S
    NB = T // BT
    NT = BT // P
    NJ = S // P
    W = 3 * I
    SH = E
    NF = NE + 1
    FC = F // P
    TW = 2 * F
    K2 = 2
    CH = FC * NF
    DOWN_LAG = 3
    GROUPS = NB + 1
    DVE_MASKS = ((1, 2, 5, 6, 8), (5,))
    Y_LAG = 4

    mask_dram = nc.dram_tensor("mask_scratch", (NB, NE * BT), F16, kind="Internal").ap()

    with ExitStack() as ctx:
        def sb(name, shape, dt=F32):
            return ctx.enter_context(nc.sbuf_tensor(name, shape, dt))

        def sem(name):
            return ctx.enter_context(nc.semaphore(name))

        ident = sb("ident", [P, P])
        ident16 = sb("ident16", [P, P], F16)
        rank_desc = sb("rank_desc", [P, NT, NE])
        neg_half = sb("neg_half", [P, NT])
        cond_sb = sb("cond_sb", [P, B, E])
        router_sb = sb("router_sb", [NE, P])
        routerT = sb("routerT", [P, NE])
        gamma_sb = sb("gamma_sb", [P, 1])
        beta_sb = sb("beta_sb", [P, 1])
        top_v = sb("top_v", [P, B, 8])
        top_i = sb("top_i", [P, B * 8], U32)
        top_d = sb("top_d", [P, B])
        top_e = sb("top_e", [P, B])
        top_s = sb("top_s", [P, B])
        mix_w = sb("mix_w", [P, B * K2])
        x_tok = sb("x_tok", [P, T])
        x16 = sb("x16", [P, 2, T], F16)
        region = sb("region", [P, NB * NE * BT // 2])
        raw = region[:, 0:3 * W].rearrange("p (s w) -> p s w", s=3)
        mask_sb = region[:, :].bitcast(F16)
        w16 = sb("w16", [P, (E + 1) * 2 * W], F16)
        f1_raw = sb("f1_raw", [P, NF * F])
        f2_raw = sb("f2_raw", [P, NF * F])
        sums = sb("sums", [P, NF * 3])
        scales = sb("scales", [P, NF * 3])
        halves = sb("halves", [P, 2, NF * 3])
        abs_junk = sb("abs_junk", [P, 2 * TW], F16)
        above = sb("above", [P, TW], F16)
        below = sb("below", [P, TW], F16)
        tern = sb("tern", [P, NF * TW], F16)
        ternT = sb("ternT", [P, NF * TW], F16)
        sc2T = sb("sc2T", [NE, P])
        g_sb = sb("g_sb", [P, 2, 2 * S])
        a_sb = sb("a_sb", [P, 2, 2 * S])
        a16 = sb("a16", [P, 4, 2, 2 * S], F16)
        shared = sb("shared", [P, T])
        c_sb = sb("c_sb", [P, BT])
        stats = sb("stats", [P, NT, 6])
        mean_sum, mean_dif, dif_sq, dif_var, sq_sum, in_var, neg_mean, shift = (
            sb(n, [P, NT]) for n in
            ("mean_sum", "mean_dif", "dif_sq", "dif_var", "sq_sum", "in_var", "neg_mean", "shift"))
        var_e = sb("var_e", [P, NT])
        rstd = sb("rstd", [P, NT])
        norm = sb("norm", [P, NT, P])
        h_sb = sb("h_sb", [P, BT])
        h16 = sb("h16", [P, 2, T], F16)
        lmax = sb("lmax", [P, NT])
        ldif = sb("ldif", [P, NT, NE])
        lth = sb("lth", [P, NT, NE])
        lden = sb("lden", [P, NT, NE])
        lex = sb("lex", [P, NT, NE])
        score = sb("score", [P, NT, NE])
        smax = sb("smax", [P, NT])
        lsum = sb("lsum", [P, NT])
        prob = sb("prob", [P, NT])
        route = sb("route", [P, NT, P])
        maskT = sb("maskT", [NE, T], F16)
        gateT = sb("gateT", [NE, T])
        w16_old = w16[:, :].rearrange("p (e h w) -> p e h w", e=E + 1, h=2)
        s16 = w16_old[:, 0:6, :, 0:BT]
        hm = w16_old[:, 0:3, :, BT:2 * BT]
        s_sb = [w16_old[:, 6 + r // 2, r % 2, 0:2 * BT].bitcast(F32) for r in range(6)]
        y_shared, y_gate = g_sb[:, 0, :], g_sb[:, 1, :]
        y_sum, out_sb = a_sb[:, 0, :], a_sb[:, 1, :]

        def bank(name):
            return ctx.enter_context(nc.psum_tensor(name, [P, 512], F32))

        ps_gate = [bank("ps_gate0"), bank("ps_gate1")]
        ps_up = [bank("ps_up0"), bank("ps_up1")]
        ps_out = [bank("ps_out0"), bank("ps_out1")]
        ps_a = bank("ps_a")
        ps_b = bank("ps_b")
        ps_b16 = ps_b[:, :].bitcast(F16)
        z_bank = [ps_gate[0], ps_up[0], ps_gate[1]]
        ps_ys, ps_yr = ps_up[1], ps_out[0]

        x_in = [sem(f"x_in{n}") for n in range(NB)]
        shared_in = [sem(f"shared_in{n}") for n in range(3)]
        expert_in = [sem("expert_in_even"), sem("expert_in_odd")]
        cond_in = sem("cond_in")
        small_in = sem("small_in")
        ffn_in = sem("ffn_in")
        const_done = sem("const_done")
        const_step = sem("const_step")
        xt_done = sem("xt_done")
        xhi_done = sem("xhi_done")
        xlo_done = sem("xlo_done")
        whi_done = sem("whi_done")
        wlo_done = sem("wlo_done")
        rt_ready = sem("rt_ready")
        rt_copied = sem("rt_copied")
        pick = sem("pick")
        pick_exp = sem("pick_exp")
        gu_done = sem("gu_done")
        gelu_done = sem("gelu_done")
        prod_done = sem("prod_done")
        ahi_done = sem("ahi_done")
        alo_done = sem("alo_done")
        down_done = sem("down_done")
        out_taken = sem("out_taken")
        t1_done = sem("t1_done")
        stats_done = sem("stats_done")
        lstep = sem("lstep")
        rstd_done = sem("rstd_done")
        norm_done = sem("norm_done")
        t2_done = sem("t2_done")
        h_done = sem("h_done")
        hhi_done = sem("hhi_done")
        hlo_done = sem("hlo_done")
        logits_done = sem("logits_done")
        rstep = sem("rstep")
        ldif_done = sem("ldif_done")
        tanh_done = sem("tanh_done")
        route_done = sem("route_done")
        routeT_done = sem("routeT_done")
        maskT_done = sem("maskT_done")
        gateT_done = sem("gateT_done")
        mask_out = sem("mask_out")
        mask_in = sem("mask_in")
        abs_done = sem("abs_done")
        thr_done = sem("thr_done")
        tstep = sem("tstep")
        tern_done = sem("tern_done")
        ternT_done = sem("ternT_done")
        ternT_copied = sem("ternT_copied")
        sc2T_done = sem("sc2T_done")
        sc2T_copied = sem("sc2T_copied")
        hm_pool = sem("hm_pool")
        hm_dve = sem("hm_dve")
        z_done = sem("z_done")
        silu_done = sem("silu_done")
        shi_act = sem("shi_act")
        shi_dve = sem("shi_dve")
        slo_done = sem("slo_done")
        y_done = sem("y_done")
        ys_taken = sem("ys_taken")
        yg_done = sem("yg_done")
        yg_copied = sem("yg_copied")
        yr_taken = sem("yr_taken")
        ysum_done = sem("ysum_done")
        yT_done = sem("yT_done")
        out_ready = sem("out_ready")
        out_stored = sem("out_stored")


        ONE_AHEAD = dict(pe=[logits_done, routeT_done, yT_done], act=[gateT_done, yg_copied],
                         dve=[out_taken, hlo_done, route_done, ysum_done, out_ready])

        block = ctx.enter_context(nc.Block())

        def w_cols(e, part, col):
            return span(e * (2 * W) + (part * W + col), P)

        def w_hi(e, col, size):
            return span(e * (2 * W) + col, size)

        def w_lo(e, col, size):
            return span(e * (2 * W) + (W + col), size)

        def spread(ap, n):
            return ap.unsqueeze(2).broadcast_to([P, ap.shape[1], n])

        def mask_tokens(engine, k, f):
            mask = mask_sb[:, span(k * (NE * BT) + (f - 1) * BT, BT)].unsqueeze(1).broadcast_to([P, 2, BT])
            return engine.tensor_tensor(hm[:, f % 3, :, :], h16[:, :, span(k * BT, BT)], mask, ALU.mult)

        def masks_done(k, f, dve):
            def here(turn, last):
                return sum((m in DVE_MASKS[turn]) == dve for m in range(1, last + 1))

            if isinstance(k, int) and k == 0:
                return here(0, f)
            return k * here(1, NE) + (here(0, NE) - here(1, NE) + here(1, f))

        def scale_of(f, c):
            return slice(3 * f + c, 3 * f + c + 1)

        def act_hi(c):
            return c % 2 == 0

        def act_hi_count(c):
            return sum(act_hi(m) for m in range(c + 1))

        ACT_HIS, DVE_HIS = act_hi_count(CH - 1), CH - act_hi_count(CH - 1)

        @block.sync
        def _(sp):
            sp.sem_inc(out_stored, 16)
            for n in range(NB):
                sp.dma_start(x_tok[:, n * BT:(n + 1) * BT].rearrange("p (b r) -> p b r", b=2),
                             x[2 * n:2 * n + 2].rearrange("b (p j) d -> p b (j d)", j=NJ)).then_inc(x_in[n], 16)

            def load_expert(e, slot):
                sp.dma_start(raw[:, slot, 0:I], g_w[e]).then_inc(expert_in[slot], 16)
                sp.dma_start(raw[:, slot, I:2 * I], u_w[e]).then_inc(expert_in[slot], 16)
                sp.dma_start(raw[:, slot, 2 * I:W].rearrange("p (c d) -> p c d", d=D),
                             d_w[e].rearrange("(c p) d -> p c d", p=P)).then_inc(expert_in[slot], 16)

            load_expert(0, 0)
            load_expert(1, 1)
            sp.dma_start(f1_raw[:, 0:F].rearrange("p (c d) -> p c d", d=D),
                         fs1.rearrange("(c p) d -> p c d", p=P)).then_inc(ffn_in, 16)
            sp.dma_start(f1_raw[:, F:].rearrange("p (c d) -> p c d", d=D),
                         fe1.rearrange("e (c p) d -> p (e c) d", p=P)).then_inc(ffn_in, 16)
            sp.dma_start(f2_raw[:, 0:F], fs2).then_inc(ffn_in, 16)
            sp.dma_start(f2_raw[:, F:].rearrange("p (e f) -> p e f", f=F),
                         fe2.rearrange("e d f -> d e f")).then_inc(ffn_in, 16)
            for e in range(2, E):
                sp.wait_ge(wlo_done, e)
                load_expert(e, e % 2)
            sp.wait_ge(wlo_done, E + 1)
            for n in range(NB):
                sp.wait_ge(maskT_done, n + 1)
                sp.dma_start(mask_dram[n].rearrange("(e t) -> e t", e=NE),
                             maskT[:, n * BT:(n + 1) * BT]).then_inc(mask_out, 16)
                sp.wait_ge(mask_out, 16 * (n + 1))
                sp.dma_start(mask_sb[:, n * NE * BT:(n + 1) * NE * BT],
                             mask_dram[n].partition_broadcast(P)).then_inc(mask_in, 16)
                sp.wait_ge(mask_in, 16 * (n + 1))
            for n in range(NB):
                sp.wait_ge(out_ready, n + 2)
                sp.dma_start(out[2 * n:2 * n + 2].rearrange("b (p j) d -> p b (j d)", j=NJ),
                             out_sb.rearrange("p (b r) -> p b r", b=2)).then_inc(out_stored, 16)
            sp.wait_ge(out_stored, 16 * NB + 16)

        @block.tensor
        def _(pe):
            for ahead in ONE_AHEAD["pe"]:
                pe.sem_inc(ahead, 1)
            def gate_up(q, e, batch):
                half, xs = q % 2, span(batch * S, S)
                for bank_, base in ((ps_gate[half], 0), (ps_up[half], I)):
                    for m in range(2):
                        col = base + (2 * half + m) * P
                        dst = bank_[:, m * S:(m + 1) * S]
                        pe.matmul(dst, w16[:, w_cols(e, 0, col)], x16[:, 0, xs], start=True, stop=False)
                        pe.matmul(dst, w16[:, w_cols(e, 0, col)], x16[:, 1, xs], start=False, stop=False)
                        last = pe.matmul(dst, w16[:, w_cols(e, 1, col)], x16[:, 0, xs], start=False, stop=True)
                last.then_inc(gu_done, 1)

            def down(d, e, dst, first, final):
                for m in range(2):
                    col = 2 * I + (2 * (d % 2) + m) * P
                    hi, lo = (a16[:, d % 4, part, m * S:(m + 1) * S] for part in range(2))
                    pe.matmul(dst, w16[:, w_cols(e, 0, col)], hi, start=first and m == 0, stop=False)
                    pe.matmul(dst, w16[:, w_cols(e, 0, col)], lo, start=False, stop=False)
                    last = pe.matmul(dst, w16[:, w_cols(e, 1, col)], hi, start=False, stop=final and m == 1)
                last.then_inc(down_done, 1)

            x_bank = [ps_out[0], ps_out[1], ps_a, ps_b]
            pe.wait_ge(const_done, 1)
            for n in range(NB):
                pe.wait_ge(x_in[n], 16)
                for t in range(NT):
                    last = pe.transpose(x_bank[n][:, t * P:(t + 1) * P], x_tok[:, (n * NT + t) * P:(n * NT + t + 1) * P], ident[:, :])
                last.then_inc(xt_done, 1)
            pe.wait_ge(small_in, 48)
            pe.transpose(ps_up[1][:, 0:NE], router_sb[:, :], ident[0:NE, 0:NE]).then_inc(rt_ready, 1)

            def shared_turn(i, first):
                for q in range(4):
                    if q == 0:
                        pe.wait_ge(xlo_done, i + 1)
                    if first and q == 0:
                        pe.wait_ge(wlo_done, 1)
                    if first and q == 1:
                        pe.wait_ge(rt_copied, 1)
                    if not first or q >= 2:
                        pe.wait_ge(prod_done, i * 4 + (q - 1))
                    gate_up(q, SH, i * 2 + q // 2)
                    d = q - DOWN_LAG
                    if first and d < 0:
                        continue
                    pe.wait_ge(alo_done, i * 4 + (d + 1))
                    if d % 2 == 0:
                        if first:
                            pe.wait_ge(xlo_done, 2)
                        else:
                            pe.wait_ge(out_taken, i * 2 + d // 2)
                    down(d, SH, ps_out[(d % 4) // 2][:, 0:S], d % 2 == 0, d % 2 == 1)

            shared_turn(0, True)
            with pe.Fori(1, B // 2) as i:
                shared_turn(i, False)

            def tern_transpose(group):
                for k, f in enumerate(group):
                    for m in range(TW // P):
                        last = pe.transpose(ps_b16[:, k * TW + m * P:k * TW + (m + 1) * P],
                                            tern[:, span(f * TW + m * P, P)], ident16[:, :])
                last.then_inc(ternT_done, 1)

            def to_tokens(n):
                pe.wait_ge(out_taken, n * 2 + (B + 3))
                for t in range(NT):
                    last = pe.transpose(ps_a[:, t * P:(t + 1) * P], c_sb[:, t * P:(t + 1) * P], ident[:, :])
                last.then_inc(t1_done, 1)

            def to_features(n):
                pe.wait_ge(norm_done, n + 1)
                for t in range(NT):
                    last = pe.transpose(ps_a[:, t * P:(t + 1) * P], norm[:, t, :], ident[:, :])
                last.then_inc(t2_done, 1)

            def logits(n, groups_copied):
                pe.wait_ge(ternT_copied, groups_copied)
                pe.wait_ge(h_done, n + 1)
                for t in range(NT):
                    last = pe.matmul(ps_b[:, t * NE:(t + 1) * NE], h_sb[:, t * P:(t + 1) * P], routerT[:, :],
                                     start=True, stop=True)
                last.then_inc(logits_done, 1)

            def route_transpose(n):
                pe.wait_ge(route_done, n + 2)
                for t in range(NT):
                    last = pe.transpose(ps_b[:, t * P:(t + 1) * P], route[:, t, :], ident[:, :])
                last.then_inc(routeT_done, 1)

            def chosen_turn(i, first=False, norming=True, routing=True):
                def chosen(turn, unit):
                    at = top_i[0:1, span(turn * 16 + (unit // 2 * 8 + unit % 2), 1)]
                    return pe.value_load(at, min_val=0, max_val=E - 1)

                here, before = [chosen(i, 0)], [SH, SH]
                for q in range(8):
                    pe.wait_ge(prod_done, i * 8 + (2 * B + q - 1))
                    gate_up(q, here[q // 2], i * 2 + q // 4)
                    if q < 2 and not first:
                        before[q] = chosen(i - 1, 2 + q)
                    if q % 2 == 1 and q < 7:
                        here.append(chosen(i, q // 2 + 1))
                    if q == 0 and routing:
                        to_features(i - 2)
                    if q == 2 and routing:
                        pe.wait_ge(gateT_done, i - 1)
                        logits(i - 2, i)
                    if q == 4 and norming:
                        to_tokens(i - 1)
                    if q == 5:
                        if not first:
                            pe.wait_ge(ternT_copied, i)
                        if routing:
                            pe.wait_ge(ldif_done, i - 1)
                        pe.wait_ge(tern_done, i * 2 + 1)
                        tern_transpose([0] if first else [i * 2 - 1, i * 2])
                    if q == 7 and routing:
                        pe.wait_ge(ternT_copied, i + 1)
                        route_transpose(i - 2)
                    d = q - DOWN_LAG
                    pe.wait_ge(alo_done, i * 8 + (2 * B + d + 1))
                    if first and d < 0:
                        if d % 2 == 0:
                            pe.wait_ge(out_taken, B + d // 2)
                        down(d, SH, ps_out[(d % 4) // 2][:, 0:S], d % 2 == 0, d % 2 == 1)
                    else:
                        if d % 4 == 0:
                            pe.wait_ge(out_taken, i * 2 + (B + d // 4))
                        e = here[d // 2] if d >= 0 else before[(d % 4) // 2]
                        down(d, e, ps_out[(d % 8) // 4][:, 0:S], d % 4 == 0, d % 4 == 3)

            pe.wait_ge(pick, 2 * B)
            pe.wait_ge(wlo_done, E + 1)
            chosen_turn(0, first=True, norming=False, routing=False)
            chosen_turn(1, routing=False)
            with pe.Fori(2, NB) as i:
                chosen_turn(i)
            at = top_i[0:1, (B - 1) * 8 + 1:(B - 1) * 8 + 2]
            last_e = pe.value_load(at, min_val=0, max_val=E - 1)
            at = top_i[0:1, (B - 1) * 8:(B - 1) * 8 + 1]
            last_e0 = pe.value_load(at, min_val=0, max_val=E - 1)

            def first_layer(k, c):
                f = c // FC
                w = ternT[:, f * TW + (c % FC) * P:f * TW + (c % FC + 1) * P]
                for part in range(2):
                    rhs = h16[:, part, span(k * BT, BT)] if f == 0 else hm[:, f % 3, part, :]
                    last = pe.matmul(z_bank[c % 3][:, :], w, rhs, start=part == 0, stop=part == 1)
                last.then_inc(z_done, 1)

            def second_layer(c):
                f = c // FC
                w = ternT[:, f * TW + F + (c % FC) * P:f * TW + F + (c % FC + 1) * P]
                dst = ps_ys if f == 0 else ps_yr
                for part in range(2):
                    last = pe.matmul(dst[:, :], w, s16[:, c % 6, part, :], start=c in (0, FC) and part == 0,
                                     stop=c in (FC - 1, CH - 1) and part == 1)
                last.then_inc(y_done, 1)

            def gate_product(n):
                pe.wait_ge(gateT_done, n + 2)
                pe.wait_ge(sc2T_copied, 1)
                pe.matmul(ps_out[1][:, :], sc2T[:, :], gateT[:, span(n * BT, BT)],
                          start=True, stop=True).then_inc(yg_done, 1)

            def y_transpose(n):
                pe.wait_ge(ysum_done, n + 2)
                for t in range(NT):
                    last = pe.transpose(ps_a[:, t * P:(t + 1) * P], y_sum[:, t * P:(t + 1) * P], ident[:, :])
                last.then_inc(yT_done, 1)

            def second_layer_turn(k, c, first):
                m = c - Y_LAG
                pe.wait_ge(slo_done, k * CH + (m + 1))
                if m == 0:
                    if first:
                        pe.wait_ge(prod_done, 4 * B + 2 * B)
                    else:
                        pe.wait_ge(ys_taken, k)
                if m == FC:
                    if first:
                        pe.wait_ge(out_taken, 2 * B)
                    else:
                        pe.wait_ge(yr_taken, k)
                second_layer(m % CH)

            def ffn_turn(k, first=False, second=False):
                for c in range(CH):
                    f = c // FC
                    if not first or c >= 3:
                        pe.wait_ge(silu_done, k * CH + (c - 2))
                    elif c != 1:
                        pe.wait_ge(prod_done, 4 * B + 2 * B - (c == 0))
                    if first and c % FC == 0:
                        pe.wait_ge(ternT_copied, (f + 1) // 2 + 1)
                    if c == 0:
                        pe.wait_ge(hlo_done, k + 2)
                    elif c % FC == 0:
                        by_dve = f in DVE_MASKS[not first]
                        pe.wait_ge(hm_dve if by_dve else hm_pool, masks_done(k, f, by_dve))
                    first_layer(k, c)
                    if first and c < 3:
                        d = c + 5
                        pe.wait_ge(alo_done, 4 * B + 2 * B - 3 + c + 1)
                        down(d, (last_e0 if d == 5 else last_e), ps_out[1][:, 0:S], False, d == 7)
                    if not first and c == 0:
                        pe.wait_ge(out_taken, 2 * B + 1)
                        pe.wait_ge(yg_copied, k)
                        gate_product(k - 1)
                    if not first and c == 8:
                        pe.wait_ge(out_ready, k)
                        y_transpose(k - 1)
                    if first:
                        if c == 0:
                            to_features(2)
                        if c == 1:
                            pe.wait_ge(gateT_done, 3)
                            pe.wait_ge(thr_done, NF)
                            pe.transpose(ps_b[0:NE, 0:P], scales[:, 5::3], ident[:, :]).then_inc(sc2T_done, 1)
                        if c == 5:
                            pe.wait_ge(sc2T_copied, 1)
                            logits(2, NB)
                        if c == 6:
                            to_tokens(3)
                        if c == 9:
                            pe.wait_ge(ldif_done, 3)
                            pe.wait_ge(tern_done, NF)
                            tern_transpose([7, 8])
                        if c == 15:
                            pe.wait_ge(ternT_copied, GROUPS)
                            route_transpose(2)
                    if second:
                        if c == 1:
                            to_features(3)
                        if c == 5:
                            pe.wait_ge(gateT_done, 4)
                            logits(3, GROUPS)
                        if c == 13:
                            route_transpose(3)
                    if not first or c >= Y_LAG:
                        second_layer_turn(k, c, first)

            ffn_turn(0, first=True)
            ffn_turn(1, second=True)
            with pe.Fori(2, NB) as k:
                ffn_turn(k)
            pe.wait_ge(yg_copied, NB)
            gate_product(NB - 1)
            for c in range(Y_LAG):
                second_layer_turn(NB, c, False)
            pe.wait_ge(out_ready, NB)
            y_transpose(NB - 1)

        @block.scalar
        def _(act):
            for ahead in ONE_AHEAD["act"]:
                act.sem_inc(ahead, 1)
            act.dma_start(cond_sb[:, :, :].rearrange("p b e -> p (b e)"),
                          cond.rearrange("b e -> (b e)").partition_broadcast(P)).then_inc(cond_in, 16)
            act.dma_start(raw[:, 2, 0:I], sg_w).then_inc(shared_in[0], 16)
            act.dma_start(raw[:, 2, I:2 * I], su_w).then_inc(shared_in[1], 16)
            act.dma_start(raw[:, 2, 2 * I:W].rearrange("p (c d) -> p c d", d=D),
                          sd_w.rearrange("(c p) d -> p c d", p=P)).then_inc(shared_in[2], 16)
            act.dma_start(router_sb[:, :], router).then_inc(small_in, 16)
            act.dma_start(gamma_sb[:, :], gamma.rearrange("(p a) -> p a", a=1)).then_inc(small_in, 16)
            act.dma_start(beta_sb[:, :], beta.rearrange("(p a) -> p a", a=1)).then_inc(small_in, 16)

            act.wait_ge(pick, 2 * B + 1)
            act.activation(top_e[:, :], top_d[:, :], ACT.Exp).then_inc(pick_exp, 1)

            x_bank = [ps_out[0], ps_out[1], ps_a, ps_b]
            for part in range(3):
                act.wait_ge(shared_in[part], 16)
                act.activation(w16[:, w_hi(SH, part * I, I)], raw[:, 2, part * I:(part + 1) * I], ACT.Copy,
                               scale=WS).then_inc(whi_done, 1)
                if part == 0:
                    for n in range(NB):
                        act.wait_ge(xt_done, n + 1)
                        act.activation(x16[:, 0, n * BT:(n + 1) * BT], x_bank[n][:, :],
                                       ACT.Copy).then_inc(xhi_done, 1)
            act.wait_ge(rt_ready, 1)
            act.activation(routerT[:, :], ps_up[1][:, 0:NE], ACT.Copy).then_inc(rt_copied, 1)

            def gelu(q):
                act.activation(g_sb[:, q % 2, :], ps_gate[q % 2][:, :], ACT.Gelu_apprx_tanh,
                               scale=1.0 / WS).then_inc(gelu_done, 1)

            def act_part_hi(q):
                act.activation(a16[:, q % 4, 0, :], a_sb[:, q % 2, :], ACT.Copy).then_inc(ahi_done, 1)

            def expert_hi(slot, e, part, loads):
                act.wait_ge(expert_in[slot], loads)
                act.activation(w16[:, w_hi(e, part * I, I)], raw[:, slot, part * I:(part + 1) * I], ACT.Copy,
                               scale=WS).then_inc(whi_done, 1)

            def shared_turn(i, first):
                for q in range(4):
                    act.wait_ge(gu_done, i * 4 + (q + 1))
                    if not first or q >= 2:
                        act.wait_ge(prod_done, i * 4 + (q - 1))
                    gelu(q)
                    expert_hi(q // 2, i * 2 + q // 2, q % 2, i * 48 + 48)
                    if not first or q >= 1:
                        act.wait_ge(prod_done, i * 4 + q)
                        if not first:
                            act.wait_ge(down_done, i * 4 + (q - 3))
                        act_part_hi(q - 1)
                    if q % 2 == 1:
                        expert_hi(q // 2, i * 2 + q // 2, 2, i * 48 + 48)

            shared_turn(0, True)
            with act.Fori(1, B // 2) as i:
                shared_turn(i, False)

            def abs_sums(f, k):
                if not isinstance(f, int) or f >= 2:
                    act.wait_ge(thr_done, f - 1)
                junk = abs_junk[:, k * TW:(k + 1) * TW]
                for c in range(FC):
                    act.activation(junk[:, c * P:(c + 1) * P], f1_raw[:, span(f * (FC * P) + c * P, P)], ACT.Abs,
                                   accum_out=sums[:, span(f * 3 + c, 1)])
                act.activation(junk[:, F:TW], f2_raw[:, span(f * F, F)], ACT.Abs,
                               accum_out=sums[:, span(f * 3 + FC, 1)]).then_inc(abs_done, 1)

            def copy_ternT(g, group):
                act.wait_ge(ternT_done, g + 1)
                act.activation(ternT[:, span(group[0] * TW, len(group) * TW)], ps_b16[:, 0:len(group) * TW],
                               ACT.Copy).then_inc(ternT_copied, 1)

            def features(n):
                act.wait_ge(t2_done, n + 1)
                act.wait_ge(logits_done, n + 1)
                act.wait_ge(hlo_done, n + 1)
                act.activation(h_sb[:, :], ps_a[:, :], ACT.Identity, bias=beta_sb[:, :],
                               scale=gamma_sb[:, :]).then_inc(h_done, 1)

            def h_hi(n):
                act.wait_ge(h_done, n + 1)
                act.activation(h16[:, 0, span(n * BT, BT)], h_sb[:, :], ACT.Copy).then_inc(hhi_done, 1)

            def normalise(n):
                act.wait_ge(rstd_done, n + 1)
                act.wait_ge(t2_done, n)
                for t in range(NT):
                    last = act.activation(norm[:, t, :], ps_a[:, t * P:(t + 1) * P], ACT.Identity,
                                          bias=shift[:, t:t + 1], scale=rstd[:, t:t + 1])
                last.then_inc(norm_done, 1)

            def half_tanh(n):
                act.wait_ge(ldif_done, n + 1)
                act.wait_ge(route_done, n + 1)
                act.activation(lth[:, :, :], ldif[:, :, :], ACT.Tanh, scale=0.5).then_inc(tanh_done, 1)

            def copy_route(n):
                act.wait_ge(routeT_done, n + 2)
                act.activation(maskT[:, span(n * BT, BT)], ps_b[0:NE, :], ACT.Copy).then_inc(maskT_done, 1)
                act.activation(gateT[:, span(n * BT, BT)], ps_b[32:32 + NE, :], ACT.Copy).then_inc(gateT_done, 1)

            def chosen_turn(i, first=False, norming=True, routing=True):
                for q in range(8):
                    act.wait_ge(gu_done, i * 8 + (2 * B + q + 1))
                    act.wait_ge(prod_done, i * 8 + (2 * B + q - 1))
                    gelu(q)
                    act.wait_ge(prod_done, i * 8 + (2 * B + q))
                    act.wait_ge(down_done, i * 8 + (2 * B + q - 4))
                    act_part_hi(q - 1)
                    if q == 0 and routing:
                        features(i - 2)
                    if q == 1 and routing:
                        h_hi(i - 2)
                    if q == 1:
                        abs_sums(i * 2 + 1, 0)
                    if q == 3:
                        abs_sums(i * 2 + 2, 1)
                    if q == 4 and routing:
                        half_tanh(i - 2)
                    if q == 5:
                        copy_ternT(i, [0] if first else [i * 2 - 1, i * 2])
                    if q == 6 and norming:
                        normalise(i - 1)
                    if q == 7 and routing:
                        copy_route(i - 2)

            act.wait_ge(small_in, 48)
            act.wait_ge(ffn_in, 64)
            abs_sums(0, 1)
            chosen_turn(0, first=True, norming=False, routing=False)
            chosen_turn(1, routing=False)
            with act.Fori(2, NB) as i:
                chosen_turn(i)

            def chunk_hi(k, c, m, early):
                if act_hi(m % CH):
                    act.wait_ge(silu_done, k * CH + (m + 1))
                    if not early:
                        act.wait_ge(y_done, k * CH + (m - 5))
                    act.activation(s16[:, m % 6, 0, :], s_sb[m % 6], ACT.Copy).then_inc(shi_act, 1)

            def ffn_turn(k, first=False, second=False):
                for c in range(CH):
                    act.wait_ge(z_done, k * CH + (c + 1))
                    if not first or c >= 6:
                        act.wait_ge(slo_done, k * CH + (c - 5))
                    f = c // FC
                    act.activation(s_sb[c % 6], z_bank[c % 3][:, :], ACT.Silu,
                                   scale=scales[:, scale_of(f, c % FC)]).then_inc(silu_done, 1)
                    if not first or c >= 1:
                        chunk_hi(k, c, c - 1, first and c < 7)
                    if not first and c == 1:
                        act.wait_ge(yg_done, k)
                        act.wait_ge(ysum_done, k)
                        act.activation(y_gate, ps_out[1][:, :], ACT.Copy).then_inc(yg_copied, 1)
                    if c == 7:
                        act.wait_ge(y_done, k * CH + FC)
                        act.wait_ge(ysum_done, k + 1)
                        act.activation(y_shared, ps_ys[:, :], ACT.Copy,
                                       scale=scales[:, scale_of(0, FC)]).then_inc(ys_taken, 1)
                    if first:
                        if c == 0:
                            features(2)
                        if c == 1:
                            h_hi(2)
                        if c == 2:
                            act.wait_ge(sc2T_done, 1)
                            act.activation(sc2T[:, :], ps_b[0:NE, 0:P], ACT.Copy).then_inc(sc2T_copied, 1)
                        if c == 7:
                            half_tanh(2)
                        if c == 10:
                            copy_ternT(4, [7, 8])
                        if c == 13:
                            normalise(3)
                        if c == 16:
                            copy_route(2)
                    if second:
                        if c == 2:
                            features(3)
                        if c == 4:
                            h_hi(3)
                        if c == 8:
                            half_tanh(3)
                        if c == 14:
                            copy_route(3)

            act.wait_ge(prod_done, 6 * B)
            act.wait_ge(down_done, 6 * B - 4)
            act_part_hi(7)
            act.wait_ge(thr_done, NF)
            ffn_turn(0, first=True)
            ffn_turn(1, second=True)
            with act.Fori(2, NB) as k:
                ffn_turn(k)
            chunk_hi(NB, 0, -1, False)
            act.wait_ge(yg_done, NB)
            act.wait_ge(ysum_done, NB)
            act.activation(y_gate, ps_out[1][:, :], ACT.Copy).then_inc(yg_copied, 1)

        @block.vector
        def _(dve):
            for ahead in ONE_AHEAD["dve"]:
                dve.sem_inc(ahead, 1)
            mix = mix_w[:, :].rearrange("p (b k) -> p b k", k=K2)
            dve.wait_ge(cond_in, 16)
            for b in range(B):
                dve.max(top_v[:, b, :], cond_sb[:, b, :]).then_inc(pick, 1)
                dve.wait_ge(pick, 2 * b + 1)
                dve.max_index(top_i[:, b * 8:(b + 1) * 8], top_v[:, b, :], cond_sb[:, b, :]).then_inc(pick, 1)
            dve.tensor_tensor(top_d[:, :], top_v[:, :, 1], top_v[:, :, 0], ALU.subtract).then_inc(pick, 1)
            dve.wait_ge(pick_exp, 1)
            dve.tensor_scalar(top_s[:, :], top_e[:, :], 1.0, None, ALU.add).then_inc(pick, 1)
            dve.wait_ge(pick, 2 * B + 2)
            dve.reciprocal(mix[:, :, 0], top_s[:, :]).then_inc(pick, 1)
            dve.wait_ge(pick, 2 * B + 3)
            dve.tensor_tensor(mix[:, :, 1], mix[:, :, 0], top_e[:, :], ALU.mult).then_inc(pick, 1)

            x_bank = [ps_out[0], ps_out[1], ps_a, ps_b]

            def weight_lo(e, slot, col, size):
                return dve.scalar_tensor_tensor(out=w16[:, w_lo(e, col, size)], in0=raw[:, slot, col:col + size],
                                                scalar=WS, in1=w16[:, w_hi(e, col, size)],
                                                op0=ALU.mult, op1=ALU.subtract)

            for part in range(3):
                dve.wait_ge(whi_done, part + 1)
                last = weight_lo(SH, 2, part * I, I)
                if part == 0:
                    for n in range(NB):
                        dve.wait_ge(xhi_done, n + 1)
                        dve.tensor_tensor(x16[:, 1, n * BT:(n + 1) * BT], x_bank[n][:, :],
                                          x16[:, 0, n * BT:(n + 1) * BT], ALU.subtract).then_inc(xlo_done, 1)
            last.then_inc(wlo_done, 1)

            def product(q, weight):
                dve.scalar_tensor_tensor(out=a_sb[:, q % 2, :], in0=g_sb[:, q % 2, :], scalar=weight,
                                         in1=ps_up[q % 2][:, :], op0=ALU.mult, op1=ALU.mult).then_inc(prod_done, 1)

            def act_part_lo(q):
                dve.tensor_tensor(a16[:, q % 4, 1, :], a_sb[:, q % 2, :], a16[:, q % 4, 0, :],
                                  ALU.subtract).then_inc(alo_done, 1)

            def take_shared(u, half, cols_at):
                dve.wait_ge(down_done, u * 2 + 2)
                dve.tensor_scalar(shared[:, span(cols_at, S)], ps_out[half][:, 0:S], 1.0 / (WS * WS), None,
                                  ALU.mult).then_inc(out_taken, 1)

            def shared_turn(i, first):
                for q in range(4):
                    dve.wait_ge(gelu_done, i * 4 + (q + 1))
                    if not first or q >= 2:
                        dve.wait_ge(alo_done, i * 4 + (q - 1))
                    product(q, 1.0)
                    e = i * 2 + q // 2
                    dve.wait_ge(whi_done, e * 3 + (q % 2 + 4))
                    weight_lo(e, q // 2, q % 2 * I, I)
                    if q % 2 == 1:
                        if not first:
                            take_shared(i * 2 + (q // 2 - 2), q // 2, i * (2 * S) + (q // 2 - 2) * S)
                        dve.wait_ge(whi_done, e * 3 + 6)
                        weight_lo(e, q // 2, 2 * I, I).then_inc(wlo_done, 1)

            shared_turn(0, True)
            with dve.Fori(1, B // 2) as i:
                shared_turn(i, False)

            def take_batch(n, b):
                dve.wait_ge(down_done, n * 8 + (2 * B + 4 * b + 4))
                if b == 0:
                    dve.wait_ge(t1_done, n)
                dve.scalar_tensor_tensor(out=c_sb[:, b * S:(b + 1) * S], in0=ps_out[b][:, 0:S],
                                         scalar=1.0 / (WS * WS), in1=shared[:, span(n * BT + b * S, S)],
                                         op0=ALU.mult, op1=ALU.add).then_inc(out_taken, 1)

            def statistics(n):
                dve.wait_ge(t1_done, n + 1)
                dve.wait_ge(rstd_done, n)
                for t in range(NT):
                    last = dve.bn_stats(stats[:, t, :], ps_a[:, t * P:(t + 1) * P])
                last.then_inc(stats_done, 1)

            def h_lo(n):
                dve.wait_ge(hhi_done, n + 1)
                dve.tensor_tensor(h16[:, 1, span(n * BT, BT)], h_sb[:, :], h16[:, 0, span(n * BT, BT)],
                                  ALU.subtract).then_inc(hlo_done, 1)

            RS = 9

            def choose(n):
                lg = ps_b[:, 0:NT * NE].rearrange("p (t e) -> p t e", e=NE)
                dve.wait_ge(logits_done, n + 2)
                dve.tensor_reduce(lmax[:, :], lg, AX, ALU.max).then_inc(rstep, 1)
                dve.wait_ge(rstep, n * RS + 1)
                dve.tensor_tensor(ldif[:, :, :], lg, spread(lmax[:, :], NE), ALU.subtract).then_inc(ldif_done, 1)
                dve.wait_ge(ldif_done, n + 1)
                dve.scalar_tensor_tensor(out=score[:, :, :], in0=ldif[:, :, :], scalar=0.0, in1=rank_desc[:, :, :],
                                         op0=ALU.is_ge, op1=ALU.mult).then_inc(rstep, 1)
                dve.wait_ge(rstep, n * RS + 2)
                dve.tensor_reduce(smax[:, :], score[:, :, :], AX, ALU.max).then_inc(rstep, 1)
                dve.wait_ge(rstep, n * RS + 3)
                dve.wait_ge(routeT_done, n + 1)
                dve.tensor_tensor(route[:, :, 0:NE], score[:, :, :], spread(smax[:, :], NE),
                                  ALU.is_equal).then_inc(rstep, 1)

            def gates(n):
                dve.wait_ge(tanh_done, n + 1)
                dve.tensor_scalar(lden[:, :, :], lth[:, :, :], -1.0, 1.0, ALU.mult, ALU.add).then_inc(rstep, 1)
                dve.wait_ge(rstep, n * RS + 5)
                dve.reciprocal(lden[:, :, :], lden[:, :, :]).then_inc(rstep, 1)
                dve.wait_ge(rstep, n * RS + 6)
                dve.scalar_tensor_tensor(out=lex[:, :, :], in0=lth[:, :, :], scalar=1.0, in1=lden[:, :, :],
                                         op0=ALU.add, op1=ALU.mult).then_inc(rstep, 1)
                dve.wait_ge(rstep, n * RS + 7)
                dve.tensor_reduce(lsum[:, :], lex[:, :, :], AX, ALU.add).then_inc(rstep, 1)
                dve.wait_ge(rstep, n * RS + 8)
                dve.reciprocal(prob[:, :], lsum[:, :]).then_inc(rstep, 1)
                dve.wait_ge(rstep, n * RS + 9)
                dve.tensor_tensor(route[:, :, 32:32 + NE], route[:, :, 0:NE], spread(prob[:, :], NE),
                                  ALU.mult).then_inc(route_done, 1)

            def chosen_turn(i, first=False, norming=True, routing=True):
                for q in range(8):
                    dve.wait_ge(gelu_done, i * 8 + (2 * B + q + 1))
                    dve.wait_ge(alo_done, i * 8 + (2 * B + q - 1))
                    product(q, mix_w[:, span(i * 4 + (q // 4 * 2 + q // 2 % 2), 1)])
                    if not first or q >= 1:
                        dve.wait_ge(ahi_done, i * 8 + (2 * B + q))
                        dve.wait_ge(down_done, i * 8 + (2 * B + q - 4))
                        act_part_lo(q - 1)
                    if first and q in (1, 3):
                        take_shared(B - 2 + q // 2, q // 2, (B - 2 + q // 2) * S)
                    if q == 2:
                        if norming:
                            take_batch(i - 1, 1)
                        if routing:
                            h_lo(i - 2)
                    if q == 3 and routing:
                        choose(i - 2)
                    if q == 4 and norming:
                        statistics(i - 1)
                    if q == 5 and routing:
                        gates(i - 2)
                    if q == 7:
                        take_batch(i, 0)

            dve.wait_ge(pick, 2 * B + 4)
            dve.wait_ge(const_done, 1)
            chosen_turn(0, first=True, norming=False, routing=False)
            chosen_turn(1, routing=False)
            with dve.Fori(2, NB) as i:
                chosen_turn(i)

            def chunk_parts(k, m, early):
                his = act_hi_count(m)
                if not early:
                    dve.wait_ge(y_done, k * CH + (m - 5))
                if act_hi(m % CH):
                    dve.wait_ge(shi_act, k * ACT_HIS + his)
                else:
                    dve.wait_ge(silu_done, k * CH + (m + 1))
                    dve.tensor_copy(s16[:, m % 6, 0, :], s_sb[m % 6]).then_inc(shi_dve, 1)
                    dve.wait_ge(shi_dve, k * DVE_HIS + (m + 1 - his))
                dve.tensor_tensor(s16[:, m % 6, 1, :], s_sb[m % 6], s16[:, m % 6, 0, :],
                                  ALU.subtract).then_inc(slo_done, 1)

            def scale_routed(n):
                dve.wait_ge(y_done, n * CH + CH)
                dve.wait_ge(yg_copied, n + 2)
                dve.tensor_tensor(y_gate, ps_yr[:, :], y_gate, ALU.mult).then_inc(yr_taken, 1)

            def add_y(n):
                dve.wait_ge(yr_taken, n + 1)
                dve.wait_ge(ys_taken, n + 1)
                dve.wait_ge(yT_done, n + 1)
                dve.tensor_tensor(y_sum, y_gate, y_shared, ALU.add).then_inc(ysum_done, 1)

            def finish(n):
                dve.wait_ge(yT_done, n + 2)
                dve.wait_ge(out_stored, n * 16 + 16)
                dve.tensor_tensor(out_sb, ps_a[:, :], x_tok[:, span(n * BT, BT)],
                                  ALU.add).then_inc(out_ready, 1)

            def ffn_turn(k, first=False, second=False):
                for c in range(CH):
                    if first and c == 0:
                        dve.wait_ge(ahi_done, 6 * B)
                        dve.wait_ge(down_done, 6 * B - 4)
                        act_part_lo(7)
                    if not first and c == 4:
                        scale_routed(k - 1)
                    if not first or c >= 1:
                        chunk_parts(k, c - 1, first and c < 7)
                    if not first and c == 5:
                        add_y(k - 1)
                    for f in DVE_MASKS[not first]:
                        if c == max(FC * f - 4, 0):
                            if first and f == 1:
                                dve.wait_ge(gu_done, 6 * B)
                                dve.wait_ge(mask_in, 16)
                            if f > 3:
                                dve.wait_ge(z_done, k * CH + (f - 2) * FC)
                            mask_tokens(dve, k, f).then_inc(hm_dve, 1)
                    if not first and c == 10:
                        finish(k - 1)
                    if first:
                        if c == 2:
                            h_lo(2)
                        if c == 3:
                            take_batch(3, 1)
                        if c == 6:
                            choose(2)
                        if c == 8:
                            statistics(3)
                        if c == 10:
                            gates(2)
                    if second:
                        if c == 5:
                            h_lo(3)
                        if c == 7:
                            choose(3)
                        if c == 9:
                            gates(3)

            ffn_turn(0, first=True)
            ffn_turn(1, second=True)
            with dve.Fori(2, NB) as k:
                ffn_turn(k)
            chunk_parts(NB, -1, False)
            scale_routed(NB - 1)
            add_y(NB - 1)
            finish(NB - 1)

        @block.gpsimd
        def _(pool):
            pool.memset(ident[:, :], 0.0).then_inc(const_step, 1)
            pool.wait_ge(const_step, 1)
            pool.affine_select(out=ident[:, :], in_=ident[:, :], compare_op=ALU.not_equal, fill=1.0, base=0,
                               pattern=[[-1, P]], channel_multiplier=1).then_inc(const_step, 1)
            pool.wait_ge(const_step, 2)
            pool.tensor_copy(ident16[:, :], ident[:, :])
            for e in range(NE):
                pool.memset(rank_desc[:, :, e], float(NE - e))
            pool.memset(neg_half[:, :], -0.5).then_inc(const_step, 1)
            pool.memset(route[:, :, :], 0.0).then_inc(const_done, 1)

            def shared_turn(i, first):
                for q in range(4):
                    pool.wait_ge(ahi_done, i * 4 + (q + 1))
                    if not first:
                        pool.wait_ge(down_done, i * 4 + (q - 3))
                    pool.tensor_tensor(a16[:, q, 1, :], a_sb[:, q % 2, :], a16[:, q, 0, :],
                                       ALU.subtract).then_inc(alo_done, 1)

            shared_turn(0, True)
            with pool.Fori(1, B // 2) as i:
                shared_turn(i, False)

            def round_weights(f):
                one, two, all3 = slice(3 * f, 3 * f + FC), scale_of(f, FC), slice(3 * f, 3 * f + 3)
                pool.wait_ge(abs_done, f + 1)
                pool.tensor_scalar(scales[:, one], sums[:, one], 1.0 / D, MIN_SCALE, ALU.mult, ALU.max)
                pool.tensor_scalar(scales[:, two], sums[:, two], 1.0 / F, MIN_SCALE, ALU.mult,
                                   ALU.max).then_inc(tstep, 1)
                pool.wait_ge(tstep, 3 * f + 1)
                for sign in range(2):
                    last = pool.tensor_scalar(halves[:, sign, all3], scales[:, all3], 0.5 - sign, None, ALU.mult)
                last.then_inc(thr_done, 1)
                pool.wait_ge(thr_done, f + 1)
                for sign, (dst, op) in enumerate(((above, ALU.is_gt), (below, ALU.is_lt))):
                    for c in range(FC):
                        n = f * FC + c
                        pool.tensor_scalar(dst[:, c * P:(c + 1) * P], f1_raw[:, n * P:(n + 1) * P],
                                           halves[:, sign, scale_of(f, c)], None, op)
                    last = pool.tensor_scalar(dst[:, F:TW], f2_raw[:, f * F:(f + 1) * F],
                                              halves[:, sign, scale_of(f, FC)], None, op)
                last.then_inc(tstep, 1)
                pool.wait_ge(tstep, 3 * f + 2)
                pool.tensor_tensor(tern[:, f * TW:(f + 1) * TW], above[:, :], below[:, :],
                                   ALU.subtract).then_inc(tern_done, 1)
                pool.wait_ge(tern_done, f + 1)
                pool.sem_inc(tstep, 1)

            def deviation(n):
                pool.wait_ge(stats_done, n + 1)
                pool.tensor_tensor(mean_sum[:, :], stats[:, :, 1], stats[:, :, 4], ALU.add)
                pool.tensor_tensor(mean_dif[:, :], stats[:, :, 1], stats[:, :, 4], ALU.subtract)
                pool.tensor_tensor(sq_sum[:, :], stats[:, :, 2], stats[:, :, 5], ALU.add).then_inc(lstep, 1)
                pool.wait_ge(lstep, 5 * n + 1)
                pool.tensor_tensor(dif_sq[:, :], mean_dif[:, :], mean_dif[:, :], ALU.mult)
                pool.tensor_scalar(neg_mean[:, :], mean_sum[:, :], -0.5, None, ALU.mult)
                pool.tensor_scalar(in_var[:, :], sq_sum[:, :], 1.0 / D, LN_EPS, ALU.mult, ALU.add).then_inc(lstep, 1)
                pool.wait_ge(lstep, 5 * n + 2)
                pool.tensor_scalar(dif_var[:, :], dif_sq[:, :], 0.25, None, ALU.mult).then_inc(lstep, 1)
                pool.wait_ge(lstep, 5 * n + 3)
                pool.tensor_tensor(var_e[:, :], in_var[:, :], dif_var[:, :], ALU.add).then_inc(lstep, 1)
                pool.wait_ge(lstep, 5 * n + 4)
                pool.wait_ge(norm_done, n)
                pool.tensor_tensor(rstd[:, :], var_e[:, :], neg_half[:, :], ALU.pow).then_inc(lstep, 1)
                pool.wait_ge(lstep, 5 * n + 5)
                pool.tensor_tensor(shift[:, :], neg_mean[:, :], rstd[:, :], ALU.mult).then_inc(rstd_done, 1)
                pool.wait_ge(rstd_done, n + 1)

            pool.wait_ge(const_step, 3)
            round_weights(0)
            for f in range(1, NF):
                round_weights(f)
                if f % 2 == 1 and f >= 3:
                    deviation(f // 2 - 1)

            def mask_turn(k, first):
                if first:
                    pool.wait_ge(gu_done, 6 * B)
                pool.wait_ge(mask_in, k * 16 + 16)
                pool.wait_ge(hlo_done, k + 2)
                for f in range(1, NF):
                    if first and f == 5:
                        deviation(NB - 1)
                    if f in DVE_MASKS[not first]:
                        continue
                    if f > 3:
                        pool.wait_ge(z_done, k * CH + (f - 2) * FC)
                    elif not first:
                        pool.wait_ge(z_done, k * CH)
                    mask_tokens(pool, k, f).then_inc(hm_pool, 1)

            mask_turn(0, True)
            with pool.Fori(1, NB) as k:
                mask_turn(k, False)


_INS = ["x", "cond_8", "L0_cond_skill_gate", "L0_cond_skill_up", "L0_cond_skill_down", "L0_cond_shared_gate",
        "L0_cond_shared_up", "L0_cond_shared_down", "L0_ffn_shared_w1", "L0_ffn_shared_w2", "L0_ffn_expert_w1",
        "L0_ffn_expert_w2", "L0_ffn_router_w", "L0_ffn_ln_gamma", "L0_ffn_ln_beta"]


def kernel(**inputs):
    import numpy as np
    import concourse.bacc as bacc
    from concourse.bass_utils import run_bass_kernel_spmd

    nc = bacc.Bacc("TRN2", target_bir_lowering=False, num_devices=1)
    arrays, args = {}, []
    for name in _INS:
        a = np.ascontiguousarray(inputs[name])
        arrays[f"in_{name}"] = a
        args.append(nc.dram_tensor(f"in_{name}", a.shape, mybir.dt.from_np(a.dtype), kind="ExternalInput").ap())
    out = nc.dram_tensor("out", arrays["in_x"].shape, F32, kind="ExternalOutput").ap()
    moe_adaln_ffn(nc, *args, out)
    r = run_bass_kernel_spmd(nc, [arrays], core_ids=[0])
    return r.results[0]["out"]
```

```python
from contextlib import ExitStack

import concourse.bass as bass
from concourse import mybir


P = 128
ALU = mybir.AluOpType
ACT = mybir.ActivationFunctionType
F32 = mybir.dt.float32
F16 = mybir.dt.float16
U32 = mybir.dt.uint32
AX = mybir.AxisListType.X

WS = 256.0
LN_EPS = 1e-5
MIN_SCALE = 1e-5


def span(start, size):
    return slice(start, start + size) if isinstance(start, int) else bass.ds(start, size)


def moe_adaln_ffn(nc, x, cond, g_w, u_w, d_w, sg_w, su_w, sd_w, fs1, fs2, fe1, fe2, router, gamma, beta, out):
    B, S, D = x.shape
    E, _, I = g_w.shape
    NE, F, _ = fe1.shape
    assert (B, S, D, E, I, NE, F) == (8, 256, P, 8, 512, 8, 256)
    T = B * S
    BT = 2 * S
    NB = T // BT
    NT = BT // P
    NJ = S // P
    W = 3 * I
    SH = E
    NF = NE + 1
    FC = F // P
    TW = 2 * F
    K2 = 2
    CH = FC * NF
    DOWN_LAG = 3
    DVE_MASKS = ((1, 2, 7, 8), (5,))
    HM = 6
    Y_LAG = 5

    mask_dram = nc.dram_tensor("mask_scratch", (NB, NE * BT), F16, kind="Internal").ap()

    with ExitStack() as ctx:
        def sb(name, shape, dt=F32):
            return ctx.enter_context(nc.sbuf_tensor(name, shape, dt))

        def sem(name):
            return ctx.enter_context(nc.semaphore(name))

        ident = sb("ident", [P, P])
        rank_desc = sb("rank_desc", [P, NT, NE])
        neg_half = sb("neg_half", [P, NT])
        cond_sb = sb("cond_sb", [P, B, E])
        router_sb = sb("router_sb", [NE, P])
        routerT = sb("routerT", [P, NE])
        gamma_sb = sb("gamma_sb", [P, 1])
        beta_sb = sb("beta_sb", [P, 1])
        top_v = sb("top_v", [P, B, 8])
        top_i = sb("top_i", [P, B * 8], U32)
        top_d = sb("top_d", [P, B])
        top_t = sb("top_t", [P, B])
        mix_w = sb("mix_w", [P, B * K2])
        x_tok = sb("x_tok", [P, T])
        x16 = sb("x16", [P, 2, T], F16)
        region = sb("region", [P, NB * NE * BT // 2])
        SH_SLOT = 4
        SLOTS = [3] + [e // 2 + 1 if e % 2 else e // 2 - 1 for e in range(1, E)]
        mask_sb = region[:, :].bitcast(F16)
        w16 = sb("w16", [P, (E + 1) * 2 * W], F16)
        f1_raw = sb("f1_raw", [P, NF * F])
        f2_raw = sb("f2_raw", [P, NF * F])
        sums = sb("sums", [P, NF * 3])
        scales = sb("scales", [P, NF * 3])
        halves = sb("halves", [P, 2, NF * 3])
        abs_junk = sb("abs_junk", [P, TW], F16)
        above = sb("above", [P, TW], F16)
        below = sb("below", [P, TW], F16)
        tern = sb("tern", [P, NF * TW], F16)
        ternT = sb("ternT", [P, NF * TW], F16)
        sc2T = sb("sc2T", [NE, P])
        g_sb = sb("g_sb", [P, 2, 2 * S])
        a_sb = sb("a_sb", [P, 2, 2 * S])
        a16 = sb("a16", [P, 4, 2, 2 * S], F16)
        shared = sb("shared", [P, T])
        c_sb = sb("c_sb", [P, BT])
        stats = sb("stats", [P, NT, 6])
        mean_sum, mean_dif, dif_sq, dif_var, sq_sum, in_var, neg_mean, shift = (
            sb(n, [P, NT]) for n in
            ("mean_sum", "mean_dif", "dif_sq", "dif_var", "sq_sum", "in_var", "neg_mean", "shift"))
        var_e = sb("var_e", [P, NT])
        rstd = sb("rstd", [P, NT])
        norm = sb("norm", [P, NT, P])
        h_sb = sb("h_sb", [P, BT])
        h16 = sb("h16", [P, 2, T], F16)
        lmax = sb("lmax", [P, NT])
        ldif = sb("ldif", [P, NT, NE])
        lth = sb("lth", [P, NT, NE])
        lden = sb("lden", [P, NT, NE])
        lex = sb("lex", [P, NT, NE])
        score = sb("score", [P, NT, NE])
        smax = sb("smax", [P, NT])
        lsum = sb("lsum", [P, NT])
        prob = sb("prob", [P, NT])
        route = sb("route", [P, NT, P])
        maskT = sb("maskT", [NE, T], F16)
        gateT = sb("gateT", [NE, T])
        w16_old = w16[:, :].rearrange("p (e h w) -> p e h w", e=E + 1, h=2)
        s16 = w16_old[:, 0:6, :, 0:BT]
        hm = w16_old[:, 0:HM, :, BT:2 * BT]
        s_sb = [w16_old[:, 6 + r // 2, r % 2, 0:2 * BT].bitcast(F32) for r in range(6)]
        y_gate = g_sb[:, 1, :]
        y_sum, out_sb = a_sb[:, 0, :], a_sb[:, 1, :]

        def bank(name):
            return ctx.enter_context(nc.psum_tensor(name, [P, 512], F32))

        ps_gate = [bank("ps_gate0"), bank("ps_gate1")]
        ps_up = [bank("ps_up0"), bank("ps_up1")]
        ps_out = [bank("ps_out0"), bank("ps_out1")]
        ps_a = bank("ps_a")
        ps_b = bank("ps_b")
        x_bank = [ps_a, ps_b, ps_a, ps_b]
        z_bank = [ps_gate[0], ps_up[0], ps_gate[1]]
        ps_ys, ps_yr = ps_up[1], ps_out[0]

        x_in = [sem(f"x_in{n}") for n in range(NB)]
        shared_in = [sem(f"shared_in{n}") for n in range(3)]
        expert_in = [sem("expert_in_even"), sem("expert_in_odd")]
        cond_in = sem("cond_in")
        small_in = sem("small_in")
        ffn_in = sem("ffn_in")
        const_done = sem("const_done")
        const_step = sem("const_step")
        xt_done = sem("xt_done")
        xhi_done = sem("xhi_done")
        xlo_done = sem("xlo_done")
        whi_done = sem("whi_done")
        e0_hi = sem("e0_hi")
        wlo_done = sem("wlo_done")
        shared_split = sem("shared_split")
        rt_ready = sem("rt_ready")
        rt_copied = sem("rt_copied")
        pick = sem("pick")
        pick_tanh = sem("pick_tanh")
        gate_done = sem("gate_done")
        gu_done = sem("gu_done")
        gelu_done = sem("gelu_done")
        prod_done = sem("prod_done")
        ahi_done = sem("ahi_done")
        alo_done = sem("alo_done")
        down_done = sem("down_done")
        out_taken = sem("out_taken")
        t1_done = sem("t1_done")
        stats_done = sem("stats_done")
        lstep = sem("lstep")
        rstd_done = sem("rstd_done")
        norm_done = sem("norm_done")
        t2_done = sem("t2_done")
        h_done = sem("h_done")
        hhi_done = sem("hhi_done")
        hlo_done = sem("hlo_done")
        logits_done = sem("logits_done")
        rstep = sem("rstep")
        ldif_done = sem("ldif_done")
        tanh_done = sem("tanh_done")
        route_done = sem("route_done")
        routeT_done = sem("routeT_done")
        maskT_done = sem("maskT_done")
        gateT_done = sem("gateT_done")
        mask_out = sem("mask_out")
        mask_in = sem("mask_in")
        abs_done = sem("abs_done")
        thr_done = sem("thr_done")
        tstep = sem("tstep")
        tern_done = sem("tern_done")
        ternT_in = sem("ternT_in")
        sc2T_done = sem("sc2T_done")
        sc2T_copied = sem("sc2T_copied")
        hm_pool = sem("hm_pool")
        hm_dve = sem("hm_dve")
        z_done = sem("z_done")
        silu_done = sem("silu_done")
        shi_act = sem("shi_act")
        shi_dve = sem("shi_dve")
        slo_done = sem("slo_done")
        y_done = sem("y_done")
        yg_done = sem("yg_done")
        yg_copied = sem("yg_copied")
        yr_taken = sem("yr_taken")
        ysum_done = sem("ysum_done")
        yT_done = sem("yT_done")
        out_ready = sem("out_ready")
        out_stored = sem("out_stored")

        ONE_AHEAD = dict(pe=[logits_done, routeT_done, yT_done], act=[maskT_done, yg_copied],
                         dve=[gateT_done, out_taken, hlo_done, route_done, ysum_done, out_ready])

        block = ctx.enter_context(nc.Block())

        def w_cols(e, part, col):
            return span(e * (2 * W) + (part * W + col), P)

        def raw_cols(slot, part):
            return region[:, span(slot * W + part * I, I)]

        def raw_down(slot):
            return raw_cols(slot, 2).rearrange("p (c d) -> p c d", d=D)

        def w_hi(e, col, size):
            return span(e * (2 * W) + col, size)

        def w_lo(e, col, size):
            return span(e * (2 * W) + (W + col), size)

        def spread(ap, n):
            return ap.unsqueeze(2).broadcast_to([P, ap.shape[1], n])

        def mask_tokens(engine, k, f):
            mask = mask_sb[:, span(k * (NE * BT) + (f - 1) * BT, BT)].unsqueeze(1).broadcast_to([P, 2, BT])
            return engine.tensor_tensor(hm[:, f % HM, :, :], h16[:, :, span(k * BT, BT)], mask, ALU.mult)

        ROUTED = FC * NE

        def expert_at(m, block0):
            return m % CH // FC if block0 else (m % CH // FC + 1) % NF

        def masks_done(k, f, dve):
            def here(turn, last):
                return sum((m in DVE_MASKS[turn]) == dve for m in range(1, last + 1))

            if isinstance(k, int) and k == 0:
                return here(0, f)
            return k * here(1, NE) + (here(0, NE) - here(1, NE) + here(1, f))

        def mask_use(k, f, second):
            return (k - 1) * CH + ((f + HM if f + HM <= NE else f) + second) * FC

        def scale_of(f, c):
            return slice(3 * f + c, 3 * f + c + 1)

        def act_hi(c):
            return c % 3 != 1

        def act_hi_count(c):
            return sum(act_hi(m) for m in range(c + 1))

        ACT_HIS, DVE_HIS = act_hi_count(CH - 1), CH - act_hi_count(CH - 1)

        @block.sync
        def _(sp):
            sp.sem_inc(out_stored, 16)
            def load_x(n):
                sp.dma_start(x_tok[:, n * BT:(n + 1) * BT].rearrange("p (b r) -> p b r", b=2),
                             x[2 * n:2 * n + 2].rearrange("b (p j) d -> p b (j d)", j=NJ)).then_inc(x_in[n], 16)

            def load_expert(e):
                slot, done = SLOTS[e], expert_in[e % 2]
                if e >= 2:
                    sp.wait_ge(done, 48 * (e // 2))
                users = [at for at in range(e) if SLOTS[at] == slot]
                if slot == SH_SLOT or users:
                    sp.wait_ge(wlo_done, max(users[-1] + 2, 3) if users else 1)
                sp.dma_start(raw_cols(slot, 0), g_w[e]).then_inc(done, 16)
                sp.dma_start(raw_cols(slot, 1), u_w[e]).then_inc(done, 16)
                sp.dma_start(raw_down(slot), d_w[e].rearrange("(c p) d -> p c d", p=P)).then_inc(done, 16)

            load_x(0)
            sp.dma_start(raw_cols(SH_SLOT, 1), su_w).then_inc(shared_in[1], 16)
            load_expert(0)
            load_x(1)
            sp.dma_start(raw_down(SH_SLOT), sd_w.rearrange("(c p) d -> p c d", p=P)).then_inc(shared_in[2], 16)
            load_x(2)
            load_x(3)
            load_expert(1)
            sp.dma_start(router_sb[:, :], router).then_inc(small_in, 16)
            sp.dma_start(gamma_sb[:, :], gamma.rearrange("(p a) -> p a", a=1)).then_inc(small_in, 16)
            sp.dma_start(beta_sb[:, :], beta.rearrange("(p a) -> p a", a=1)).then_inc(small_in, 16)
            for e in range(2, E):
                load_expert(e)
                if e == 3:
                    sp.dma_start(f1_raw[:, 0:F].rearrange("p (c d) -> p c d", d=D),
                                 fs1.rearrange("(c p) d -> p c d", p=P)).then_inc(ffn_in, 16)
                    sp.dma_start(f2_raw[:, 0:F], fs2).then_inc(ffn_in, 16)
                if e == 4:
                    sp.dma_start(f1_raw[:, F:].rearrange("p (c d) -> p c d", d=D),
                                 fe1.rearrange("e (c p) d -> p (e c) d", p=P)).then_inc(ffn_in, 16)
                if e == 6:
                    sp.dma_start(f2_raw[:, F:].rearrange("p (e f) -> p e f", f=F),
                                 fe2.rearrange("e d f -> d e f")).then_inc(ffn_in, 16)
            sp.wait_ge(wlo_done, E + 1)

            def transpose_ternary(f):
                sp.wait_ge(tern_done, f + 1)
                for m in range(TW // P):
                    at = f * TW + m * P
                    sp.dma_start(ternT[:, at:at + P], tern[:, at:at + P], transpose=True).then_inc(ternT_in, 16)
                sp.wait_ge(ternT_in, TW // P * 16 * (f + 1))

            def spread_mask(n):
                sp.wait_ge(maskT_done, n + 2)
                sp.dma_start(mask_dram[n].rearrange("(e t) -> e t", e=NE),
                             maskT[:, n * BT:(n + 1) * BT]).then_inc(mask_out, 16)
                sp.wait_ge(mask_out, 16 * (n + 1))
                sp.dma_start(mask_sb[:, n * NE * BT:(n + 1) * NE * BT],
                             mask_dram[n].partition_broadcast(P)).then_inc(mask_in, 16)
                sp.wait_ge(mask_in, 16 * (n + 1))

            for f in range(NF):
                transpose_ternary(f)
                if f in (5, 7):
                    spread_mask((f - 5) // 2)
            spread_mask(2)
            spread_mask(3)
            for n in range(NB - 1):
                sp.wait_ge(out_ready, n + 2)
                sp.dma_start(out[2 * n:2 * n + 2].rearrange("b (p j) d -> p b (j d)", j=NJ),
                             out_sb.rearrange("p (b r) -> p b r", b=2)).then_inc(out_stored, 16)
            for half in range(2):
                sp.wait_ge(out_ready, NB + 1 + half)
                sp.dma_start(out[B - 2 + half].rearrange("(p j) d -> p (j d)", j=NJ),
                             out_sb[:, half * S:half * S + S]).then_inc(out_stored, 16)
            sp.wait_ge(out_stored, 16 * (NB + 1) + 16)

        @block.tensor
        def _(pe):
            for ahead in ONE_AHEAD["pe"]:
                pe.sem_inc(ahead, 1)
            def gate_up(q, e, batch, before, splits=False):
                half, xs = q % 2, span(batch * S, S)
                for bank_, base, used, done in ((ps_gate[half], 0, gelu_done, gate_done),
                                                (ps_up[half], I, prod_done, gu_done)):
                    if before is not None:
                        pe.wait_ge(used, before)
                    if splits:
                        pe.wait_ge(shared_split, 1 + base // I)
                    for m in range(2):
                        col = base + (2 * half + m) * P
                        dst = bank_[:, m * S:(m + 1) * S]
                        pe.matmul(dst, w16[:, w_cols(e, 0, col)], x16[:, 0, xs], start=True, stop=False)
                        pe.matmul(dst, w16[:, w_cols(e, 0, col)], x16[:, 1, xs], start=False, stop=False)
                        last = pe.matmul(dst, w16[:, w_cols(e, 1, col)], x16[:, 0, xs], start=False, stop=True)
                    last.then_inc(done, 1)

            def down(d, e, dst, first, final):
                for m in range(2):
                    col = 2 * I + (2 * (d % 2) + m) * P
                    hi, lo = (a16[:, d % 4, part, m * S:(m + 1) * S] for part in range(2))
                    pe.matmul(dst, w16[:, w_cols(e, 0, col)], hi, start=first and m == 0, stop=False)
                    pe.matmul(dst, w16[:, w_cols(e, 0, col)], lo, start=False, stop=False)
                    last = pe.matmul(dst, w16[:, w_cols(e, 1, col)], hi, start=False, stop=final and m == 1)
                last.then_inc(down_done, 1)

            def x_transpose(n):
                pe.wait_ge(x_in[n], 16)
                if n >= 2:
                    pe.wait_ge(xlo_done, n - 1)
                for t in range(NT):
                    last = pe.transpose(x_bank[n][:, t * P:(t + 1) * P],
                                        x_tok[:, (n * NT + t) * P:(n * NT + t + 1) * P], ident[:, :])
                last.then_inc(xt_done, 1)

            pe.wait_ge(const_done, 1)
            x_transpose(0)

            def shared_turn(i, first):
                for q in range(4):
                    if q == 0:
                        pe.wait_ge(xlo_done, i + 1)
                    gate_up(q, SH, i * 2 + q // 2, None if first and q < 2 else i * 4 + (q - 1), first and q == 0)
                    if first and q < 3:
                        x_transpose(q + 1)
                    d = q - DOWN_LAG
                    if first and d < 0:
                        continue
                    pe.wait_ge(alo_done, i * 4 + (d + 1))
                    if d % 2 == 0:
                        if first:
                            pe.wait_ge(wlo_done, 1)
                        else:
                            pe.wait_ge(out_taken, i * 2 + d // 2)
                    down(d, SH, ps_out[(d % 4) // 2][:, 0:S], d % 2 == 0, d % 2 == 1)

            shared_turn(0, True)
            with pe.Fori(1, B // 2) as i:
                shared_turn(i, False)

            def to_tokens(n):
                pe.wait_ge(out_taken, n * 2 + (B + 3))
                for t in range(NT):
                    last = pe.transpose(ps_a[:, t * P:(t + 1) * P], c_sb[:, t * P:(t + 1) * P], ident[:, :])
                last.then_inc(t1_done, 1)

            def to_features(n):
                pe.wait_ge(norm_done, n + 1)
                for t in range(NT):
                    last = pe.transpose(ps_a[:, t * P:(t + 1) * P], norm[:, t, :], ident[:, :])
                last.then_inc(t2_done, 1)

            def logits(n):
                pe.wait_ge(rt_copied, 1)
                pe.wait_ge(h_done, n + 1)
                for t in range(NT):
                    last = pe.matmul(ps_b[:, t * NE:(t + 1) * NE], h_sb[:, t * P:(t + 1) * P], routerT[:, :],
                                     start=True, stop=True)
                last.then_inc(logits_done, 1)

            def route_transpose(n):
                pe.wait_ge(route_done, n + 2)
                for t in range(NT):
                    last = pe.transpose(ps_b[:, t * P:(t + 1) * P], route[:, t, :], ident[:, :])
                last.then_inc(routeT_done, 1)

            def chosen_turn(i, first=False, norming=True, routing=True):
                def chosen(turn, unit):
                    at = top_i[0:1, span(turn * 16 + (unit // 2 * 8 + unit % 2), 1)]
                    return pe.value_load(at, min_val=0, max_val=E - 1)

                here, before = [chosen(i, 0)], [SH, SH]
                for q in range(8):
                    gate_up(q, here[q // 2], i * 2 + q // 4, i * 8 + (2 * B + q - 1))
                    if q == 1 and routing:
                        to_features(i - 2)
                    if q < 2 and not first:
                        before[q] = chosen(i - 1, 2 + q)
                    if q == 3 and routing:
                        pe.wait_ge(maskT_done, i - 1)
                        pe.wait_ge(gateT_done, i - 1)
                        logits(i - 2)
                    if q == 4 and norming:
                        to_tokens(i - 1)
                    if q == 7 and routing:
                        route_transpose(i - 2)
                    d = q - DOWN_LAG
                    pe.wait_ge(alo_done, i * 8 + (2 * B + d + 1))
                    if first and d < 0:
                        if d % 2 == 0:
                            pe.wait_ge(out_taken, B + d // 2)
                        down(d, SH, ps_out[(d % 4) // 2][:, 0:S], d % 2 == 0, d % 2 == 1)
                    else:
                        if d % 4 == 0:
                            pe.wait_ge(out_taken, i * 2 + (B + d // 4))
                        e = here[d // 2] if d >= 0 else before[(d % 4) // 2]
                        down(d, e, ps_out[(d % 8) // 4][:, 0:S], d % 4 == 0, d % 4 == 3)
                    if q % 2 == 1 and q < 7:
                        here.append(chosen(i, q // 2 + 1))

            pe.wait_ge(xlo_done, NB)
            pe.wait_ge(small_in, 48)
            pe.transpose(ps_b[:, 0:NE], router_sb[:, :], ident[0:NE, 0:NE]).then_inc(rt_ready, 1)

            pe.wait_ge(pick, 2 * B)
            pe.wait_ge(wlo_done, E + 1)
            chosen_turn(0, first=True, norming=False, routing=False)
            chosen_turn(1, routing=False)
            with pe.Fori(2, NB) as i:
                chosen_turn(i)
            at = top_i[0:1, (B - 1) * 8 + 1:(B - 1) * 8 + 2]
            last_e = pe.value_load(at, min_val=0, max_val=E - 1)
            at = top_i[0:1, (B - 1) * 8:(B - 1) * 8 + 1]
            last_e0 = pe.value_load(at, min_val=0, max_val=E - 1)

            def first_layer(k, c, f):
                w = ternT[:, f * TW + (c % FC) * P:f * TW + (c % FC + 1) * P]
                for part in range(2):
                    rhs = h16[:, part, span(k * BT, BT)] if f == 0 else hm[:, f % HM, part, :]
                    last = pe.matmul(z_bank[c % 3][:, :], w, rhs, start=part == 0, stop=part == 1)
                last.then_inc(z_done, 1)

            def second_layer(m, block0):
                f = expert_at(m, block0)
                w = ternT[:, f * TW + F + (m % FC) * P:f * TW + F + (m % FC + 1) * P]
                dst, chunks = (ps_ys, FC) if f == 0 else (ps_yr, ROUTED)
                first_chunk = (0 if f == 0 else FC) if block0 else (ROUTED if f == 0 else 0)
                for part in range(2):
                    last = pe.matmul(dst[:, :], w, s16[:, m % 6, part, :], start=m == first_chunk and part == 0,
                                     stop=m == first_chunk + chunks - 1 and part == 1)
                last.then_inc(y_done, 1)

            def gate_product(n):
                pe.wait_ge(gateT_done, n + 2)
                pe.wait_ge(sc2T_copied, 1)
                pe.matmul(ps_out[1][:, :], sc2T[:, :], gateT[:, span(n * BT, BT)],
                          start=True, stop=True).then_inc(yg_done, 1)

            def y_transpose(n):
                pe.wait_ge(ysum_done, n + 2)
                for t in range(NT):
                    last = pe.transpose(ps_a[:, t * P:(t + 1) * P], y_sum[:, t * P:(t + 1) * P], ident[:, :])
                last.then_inc(yT_done, 1)

            def second_layer_turn(k, c, first=False, second=False):
                m = c - Y_LAG
                pe.wait_ge(slo_done, k * CH + (m + 1))
                if first and m == 0:
                    pe.wait_ge(prod_done, 4 * B + 2 * B)
                if first and m == FC:
                    pe.wait_ge(out_taken, 2 * B)
                if not first and m == 0:
                    pe.wait_ge(yr_taken, k)
                if not first and not second and m == ROUTED - CH:
                    pe.wait_ge(ysum_done, k)
                second_layer(m % CH, first or (second and m < 0))

            def ffn_turn(k, first=False, second=False):
                for c in range(CH):
                    f = expert_at(c, first)
                    if not first or c >= 3:
                        pe.wait_ge(silu_done, k * CH + (c - 2))
                    elif c != 1:
                        pe.wait_ge(prod_done, 4 * B + 2 * B - (c == 0))
                    if first and c % FC == 0:
                        pe.wait_ge(ternT_in, TW // P * 16 * (f + 1))
                    if c == 0:
                        pe.wait_ge(hlo_done, k + 2)
                    if f != 0 and c % FC == 0:
                        by_dve = f in DVE_MASKS[not first]
                        pe.wait_ge(hm_dve if by_dve else hm_pool, masks_done(k, f, by_dve))
                    first_layer(k, c, f)
                    if first and c < 3:
                        d = c + 5
                        pe.wait_ge(alo_done, 4 * B + 2 * B - 3 + c + 1)
                        down(d, (last_e0 if d == 5 else last_e), ps_out[1][:, 0:S], False, d == 7)
                    if not first and c == 0:
                        pe.wait_ge(out_taken, 2 * B + 1)
                        pe.wait_ge(yg_copied, k)
                        gate_product(k - 1)
                    if not first and c == 10:
                        pe.wait_ge(out_ready, k)
                        y_transpose(k - 1)
                    if first:
                        if c == 0:
                            to_features(2)
                        if c == 1:
                            pe.wait_ge(maskT_done, 3)
                            pe.wait_ge(gateT_done, 3)
                            pe.wait_ge(thr_done, NF)
                            pe.transpose(ps_b[0:NE, 0:P], scales[:, 5::3], ident[:, :]).then_inc(sc2T_done, 1)
                        if c == 5:
                            pe.wait_ge(sc2T_copied, 1)
                            logits(2)
                        if c == 6:
                            to_tokens(3)
                        if c == 17:
                            route_transpose(2)
                    if second:
                        if c == 1:
                            to_features(3)
                        if c == 5:
                            pe.wait_ge(maskT_done, 4)
                            pe.wait_ge(gateT_done, 4)
                            logits(3)
                        if c == 15:
                            route_transpose(3)
                    if not first or c >= Y_LAG:
                        second_layer_turn(k, c, first, second)

            ffn_turn(0, first=True)
            ffn_turn(1, second=True)
            with pe.Fori(2, NB) as k:
                ffn_turn(k)
            pe.wait_ge(yg_copied, NB)
            gate_product(NB - 1)
            for c in range(Y_LAG):
                second_layer_turn(NB, c)
            pe.wait_ge(out_ready, NB)
            pe.wait_ge(maskT_done, NB + 1)
            pe.wait_ge(gateT_done, NB + 1)
            for half, dst in enumerate((ps_a, ps_b)):
                pe.wait_ge(ysum_done, NB + 1 + half)
                for t in range(NJ):
                    at = half * S + t * P
                    last = pe.transpose(dst[:, t * P:(t + 1) * P], y_sum[:, at:at + P], ident[:, :])
                last.then_inc(yT_done, 1)

        @block.scalar
        def _(act):
            for ahead in ONE_AHEAD["act"]:
                act.sem_inc(ahead, 1)
            act.dma_start(raw_cols(SH_SLOT, 0), sg_w).then_inc(shared_in[0], 16)
            act.dma_start(cond_sb[:, :, :].rearrange("p b e -> p (b e)"),
                          cond.rearrange("b e -> (b e)").partition_broadcast(P)).then_inc(cond_in, 16)
            act.wait_ge(const_step, 3)
            act.activation(shift[:, :], neg_half[:, :], ACT.Gelu_apprx_tanh)

            def shared_hi(part):
                act.wait_ge(shared_in[part], 16)
                act.activation(w16[:, w_hi(SH, part * I, I)], raw_cols(SH_SLOT, part), ACT.Copy,
                               scale=WS).then_inc(whi_done, 1)

            def x_hi(n):
                act.wait_ge(xt_done, n + 1)
                act.activation(x16[:, 0, n * BT:(n + 1) * BT], x_bank[n][:, :], ACT.Copy).then_inc(xhi_done, 1)

            def expert_hi(e, slot, part, done, loads):
                act.wait_ge(expert_in[done], loads)
                act.activation(w16[:, w_hi(e, part * I, I)], raw_cols(slot, part), ACT.Copy,
                               scale=WS).then_inc(whi_done, 1)

            shared_hi(0)
            x_hi(0)
            shared_hi(1)

            def gelu(q):
                act.activation(g_sb[:, q % 2, :], ps_gate[q % 2][:, :], ACT.Gelu_apprx_tanh,
                               scale=1.0 / WS).then_inc(gelu_done, 1)

            def act_part_hi(q):
                act.activation(a16[:, q % 4, 0, :], a_sb[:, q % 2, :], ACT.Copy).then_inc(ahi_done, 1)

            def shared_turn(i, first=False, final=False):
                for q in range(4):
                    act.wait_ge(gate_done, i * 4 + (q + 1))
                    if not first or q >= 2:
                        act.wait_ge(prod_done, i * 4 + (q - 1))
                    gelu(q)
                    if not first or q >= 1:
                        act.wait_ge(prod_done, i * 4 + q)
                        if not first:
                            act.wait_ge(down_done, i * 4 + (q - 3))
                        act_part_hi(q - 1)
                    if first and q == 1:
                        expert_hi(1, SLOTS[1], 0, 1, 48)
                    if first and q < 3:
                        x_hi(q + 1)
                    if first and q == 1:
                        shared_hi(2)
                    if first and q == 2:
                        act.wait_ge(pick, 2 * B + 1)
                        act.activation(top_t[:, :], top_d[:, :], ACT.Tanh, scale=0.5).then_inc(pick_tanh, 1)
                    e, slot = i * 2 + (q // 2 + 1), i + (q < 2)
                    done, loads = int(q < 2), i * 48 + (48 + q // 2 * 48)
                    if (not final or q < 2) and not (first and q == 0):
                        expert_hi(e, slot, q % 2, done, loads)
                    if q % 2 == 1 and (not final or q < 2):
                        expert_hi(e, slot, 2, done, loads)

            shared_turn(0, first=True)
            with act.Fori(1, B // 2 - 1) as i:
                shared_turn(i)
            shared_turn(B // 2 - 1, final=True)

            def abs_sums(f):
                if not isinstance(f, int) or f >= 1:
                    act.wait_ge(abs_done, f)
                for c in range(FC):
                    act.activation(abs_junk[:, c * P:(c + 1) * P], f1_raw[:, span(f * (FC * P) + c * P, P)], ACT.Abs,
                                   accum_out=sums[:, span(f * 3 + c, 1)])
                act.activation(abs_junk[:, F:TW], f2_raw[:, span(f * F, F)], ACT.Abs,
                               accum_out=sums[:, span(f * 3 + FC, 1)]).then_inc(abs_done, 1)

            def features(n):
                act.wait_ge(t2_done, n + 1)
                act.wait_ge(logits_done, n + 1)
                act.wait_ge(hlo_done, n + 1)
                act.activation(h_sb[:, :], ps_a[:, :], ACT.Identity, bias=beta_sb[:, :],
                               scale=gamma_sb[:, :]).then_inc(h_done, 1)

            def h_hi(n):
                act.wait_ge(h_done, n + 1)
                act.activation(h16[:, 0, span(n * BT, BT)], h_sb[:, :], ACT.Copy).then_inc(hhi_done, 1)

            def normalise(n):
                act.wait_ge(rstd_done, n + 1)
                act.wait_ge(t2_done, n)
                for t in range(NT):
                    last = act.activation(norm[:, t, :], ps_a[:, t * P:(t + 1) * P], ACT.Identity,
                                          bias=shift[:, t:t + 1], scale=rstd[:, t:t + 1])
                last.then_inc(norm_done, 1)

            def half_tanh(n):
                act.wait_ge(ldif_done, n + 1)
                act.wait_ge(route_done, n + 1)
                act.activation(lth[:, :, :], ldif[:, :, :], ACT.Tanh, scale=0.5).then_inc(tanh_done, 1)

            def copy_choice(n):
                act.wait_ge(routeT_done, n + 2)
                act.activation(maskT[:, span(n * BT, BT)], ps_b[0:NE, :], ACT.Copy).then_inc(maskT_done, 1)

            def chosen_turn(i, first=False, norming=True, routing=True):
                for q in range(8):
                    act.wait_ge(gate_done, i * 8 + (2 * B + q + 1))
                    act.wait_ge(prod_done, i * 8 + (2 * B + q - 1))
                    gelu(q)
                    act.wait_ge(prod_done, i * 8 + (2 * B + q))
                    act.wait_ge(down_done, i * 8 + (2 * B + q - 4))
                    act_part_hi(q - 1)
                    if q == 1 and routing:
                        features(i - 2)
                    if q == 2 and routing:
                        h_hi(i - 2)
                    if not routing and q in (1, 3, 5):
                        abs_sums(3 * i + q // 2 + 1)
                    if routing and q == 3:
                        abs_sums(i + 5)
                    if q == 4 and routing:
                        half_tanh(i - 2)
                    if q == 7 and norming:
                        normalise(i - 1)
                    if q == 7 and routing:
                        copy_choice(i - 2)

            act.wait_ge(small_in, 48)
            act.wait_ge(ffn_in, 64)
            act.wait_ge(rt_ready, 1)
            act.activation(routerT[:, :], ps_b[:, 0:NE], ACT.Copy).then_inc(rt_copied, 1)
            abs_sums(0)
            chosen_turn(0, first=True, norming=False, routing=False)
            chosen_turn(1, routing=False)
            with act.Fori(2, NB) as i:
                chosen_turn(i)

            def chunk_hi(k, m, early):
                if act_hi(m % CH):
                    act.wait_ge(silu_done, k * CH + (m + 1))
                    if not early:
                        act.wait_ge(y_done, k * CH + (m - 5))
                    act.activation(s16[:, m % 6, 0, :], s_sb[m % 6], ACT.Copy).then_inc(shi_act, 1)

            def ffn_turn(k, first=False, second=False):
                for c in range(CH):
                    act.wait_ge(z_done, k * CH + (c + 1))
                    if not first or c >= 6:
                        act.wait_ge(slo_done, k * CH + (c - 5))
                    f = expert_at(c, first)
                    act.activation(s_sb[c % 6], z_bank[c % 3][:, :], ACT.Silu,
                                   scale=scales[:, scale_of(f, c % FC)]).then_inc(silu_done, 1)
                    if not first or c >= 1:
                        chunk_hi(k, c - 1, first and c < 7)
                    if not first and c == 1:
                        act.wait_ge(yg_done, k)
                        act.wait_ge(ysum_done, k)
                        act.activation(y_gate, ps_out[1][:, :], ACT.Copy).then_inc(yg_copied, 1)
                    if first:
                        if c == 0:
                            features(2)
                        if c == 1:
                            h_hi(2)
                        if c == 2:
                            act.wait_ge(sc2T_done, 1)
                            act.activation(sc2T[:, :], ps_b[0:NE, 0:P], ACT.Copy).then_inc(sc2T_copied, 1)
                        if c == 7:
                            half_tanh(2)
                        if c == 13:
                            normalise(3)
                        if c == 17:
                            copy_choice(2)
                    if second:
                        if c == 2:
                            features(3)
                        if c == 4:
                            h_hi(3)
                        if c == 8:
                            half_tanh(3)
                        if c == 16:
                            copy_choice(3)

            act.wait_ge(thr_done, NF)
            ffn_turn(0, first=True)
            ffn_turn(1, second=True)
            with act.Fori(2, NB) as k:
                ffn_turn(k)
            chunk_hi(NB, -1, False)
            act.wait_ge(yg_done, NB)
            act.wait_ge(ysum_done, NB)
            act.activation(y_gate, ps_out[1][:, :], ACT.Copy).then_inc(yg_copied, 1)

        @block.vector
        def _(dve):
            for ahead in ONE_AHEAD["dve"]:
                dve.sem_inc(ahead, 1)
            def weight_lo(e, slot, part):
                return dve.scalar_tensor_tensor(out=w16[:, w_lo(e, part * I, I)], in0=raw_cols(slot, part),
                                                scalar=WS, in1=w16[:, w_hi(e, part * I, I)],
                                                op0=ALU.mult, op1=ALU.subtract)

            def x_lo(n):
                dve.wait_ge(xhi_done, n + 1)
                dve.tensor_tensor(x16[:, 1, n * BT:(n + 1) * BT], x_bank[n][:, :], x16[:, 0, n * BT:(n + 1) * BT],
                                  ALU.subtract).then_inc(xlo_done, 1)

            for part in range(2):
                dve.wait_ge(whi_done, part + 1)
                weight_lo(SH, SH_SLOT, part).then_inc(shared_split, 1)
                if part == 0:
                    x_lo(0)

            mix = mix_w[:, :].rearrange("p (b k) -> p b k", k=K2)
            dve.wait_ge(cond_in, 16)
            for b in range(B):
                dve.max(top_v[:, b, :], cond_sb[:, b, :]).then_inc(pick, 1)
                dve.wait_ge(pick, 2 * b + 1)
                dve.max_index(top_i[:, b * 8:(b + 1) * 8], top_v[:, b, :], cond_sb[:, b, :]).then_inc(pick, 1)
            dve.tensor_tensor(top_d[:, :], top_v[:, :, 1], top_v[:, :, 0], ALU.subtract).then_inc(pick, 1)

            def product(q, weight):
                dve.scalar_tensor_tensor(out=a_sb[:, q % 2, :], in0=g_sb[:, q % 2, :], scalar=weight,
                                         in1=ps_up[q % 2][:, :], op0=ALU.mult, op1=ALU.mult).then_inc(prod_done, 1)

            def act_part_lo(q):
                dve.tensor_tensor(a16[:, q % 4, 1, :], a_sb[:, q % 2, :], a16[:, q % 4, 0, :],
                                  ALU.subtract).then_inc(alo_done, 1)

            def take_shared(u, half, cols_at):
                dve.wait_ge(down_done, u * 2 + 2)
                dve.tensor_scalar(shared[:, span(cols_at, S)], ps_out[half][:, 0:S], 1.0 / (WS * WS), None,
                                  ALU.mult).then_inc(out_taken, 1)

            def shared_turn(i, first=False, final=False):
                for q in range(4):
                    dve.wait_ge(gelu_done, i * 4 + (q + 1))
                    dve.wait_ge(gu_done, i * 4 + (q + 1))
                    if not first or q >= 2:
                        dve.wait_ge(alo_done, i * 4 + (q - 1))
                    product(q, 1.0)
                    if first and q == 2:
                        dve.wait_ge(e0_hi, 1)
                        for part in range(3):
                            last = weight_lo(0, SLOTS[0], part)
                        last.then_inc(wlo_done, 1)
                    if first and q == 1:
                        dve.wait_ge(whi_done, 3)
                        weight_lo(1, SLOTS[1], 0)
                    if first and q < 3:
                        x_lo(q + 1)
                    if first and q == 1:
                        dve.wait_ge(whi_done, 4)
                        weight_lo(SH, SH_SLOT, 2).then_inc(wlo_done, 1)
                    if first and q == 3:
                        dve.wait_ge(pick_tanh, 1)
                        for choice, sign in enumerate((-0.5, 0.5)):
                            last = dve.tensor_scalar(mix[:, :, choice], top_t[:, :], sign, 0.5, ALU.mult, ALU.add)
                        last.then_inc(pick, 1)
                    e, slot = i * 2 + (q // 2 + 1), i + (q < 2)
                    if (not final or q < 2) and not (first and q == 0):
                        dve.wait_ge(whi_done, e * 3 + (q % 2 + 1))
                        weight_lo(e, slot, q % 2)
                    if q % 2 == 1:
                        if not first:
                            take_shared(i * 2 + (q // 2 - 2), q // 2, i * (2 * S) + (q // 2 - 2) * S)
                        if not final or q < 2:
                            dve.wait_ge(whi_done, e * 3 + 3)
                            weight_lo(e, slot, 2).then_inc(wlo_done, 1)

            shared_turn(0, first=True)
            with dve.Fori(1, B // 2 - 1) as i:
                shared_turn(i)
            shared_turn(B // 2 - 1, final=True)

            def take_batch(n, b):
                dve.wait_ge(down_done, n * 8 + (2 * B + 4 * b + 4))
                if b == 0:
                    dve.wait_ge(t1_done, n)
                dve.scalar_tensor_tensor(out=c_sb[:, b * S:(b + 1) * S], in0=ps_out[b][:, 0:S],
                                         scalar=1.0 / (WS * WS), in1=shared[:, span(n * BT + b * S, S)],
                                         op0=ALU.mult, op1=ALU.add).then_inc(out_taken, 1)

            def statistics(n):
                dve.wait_ge(t1_done, n + 1)
                dve.wait_ge(rstd_done, n)
                for t in range(NT):
                    last = dve.bn_stats(stats[:, t, :], ps_a[:, t * P:(t + 1) * P])
                last.then_inc(stats_done, 1)

            def h_lo(n):
                dve.wait_ge(hhi_done, n + 1)
                dve.tensor_tensor(h16[:, 1, span(n * BT, BT)], h_sb[:, :], h16[:, 0, span(n * BT, BT)],
                                  ALU.subtract).then_inc(hlo_done, 1)

            RS = 9

            def choose(n):
                lg = ps_b[:, 0:NT * NE].rearrange("p (t e) -> p t e", e=NE)
                dve.wait_ge(logits_done, n + 2)
                dve.tensor_reduce(lmax[:, :], lg, AX, ALU.max).then_inc(rstep, 1)
                dve.wait_ge(rstep, n * RS + 1)
                dve.tensor_tensor(ldif[:, :, :], lg, spread(lmax[:, :], NE), ALU.subtract).then_inc(ldif_done, 1)
                dve.wait_ge(ldif_done, n + 1)
                dve.scalar_tensor_tensor(out=score[:, :, :], in0=ldif[:, :, :], scalar=0.0, in1=rank_desc[:, :, :],
                                         op0=ALU.is_ge, op1=ALU.mult).then_inc(rstep, 1)
                dve.wait_ge(rstep, n * RS + 2)
                dve.tensor_reduce(smax[:, :], score[:, :, :], AX, ALU.max).then_inc(rstep, 1)
                dve.wait_ge(rstep, n * RS + 3)
                dve.wait_ge(routeT_done, n + 1)
                dve.tensor_tensor(route[:, :, 0:NE], score[:, :, :], spread(smax[:, :], NE),
                                  ALU.is_equal).then_inc(rstep, 1)

            def gates(n):
                dve.wait_ge(tanh_done, n + 1)
                dve.tensor_scalar(lden[:, :, :], lth[:, :, :], -1.0, 1.0, ALU.mult, ALU.add).then_inc(rstep, 1)
                dve.wait_ge(rstep, n * RS + 5)
                dve.reciprocal(lden[:, :, :], lden[:, :, :]).then_inc(rstep, 1)
                dve.wait_ge(rstep, n * RS + 6)
                dve.scalar_tensor_tensor(out=lex[:, :, :], in0=lth[:, :, :], scalar=1.0, in1=lden[:, :, :],
                                         op0=ALU.add, op1=ALU.mult).then_inc(rstep, 1)
                dve.wait_ge(rstep, n * RS + 7)
                dve.tensor_reduce(lsum[:, :], lex[:, :, :], AX, ALU.add).then_inc(rstep, 1)
                dve.wait_ge(rstep, n * RS + 8)
                dve.reciprocal(prob[:, :], lsum[:, :]).then_inc(rstep, 1)
                dve.wait_ge(rstep, n * RS + 9)
                dve.tensor_tensor(route[:, :, 32:32 + NE], route[:, :, 0:NE], spread(prob[:, :], NE),
                                  ALU.mult).then_inc(route_done, 1)

            def copy_gates(n):
                dve.wait_ge(routeT_done, n + 2)
                dve.tensor_copy(gateT[:, span(n * BT, BT)], ps_b[32:32 + NE, :]).then_inc(gateT_done, 1)

            def chosen_turn(i, first=False, norming=True, routing=True):
                for q in range(8):
                    dve.wait_ge(gelu_done, i * 8 + (2 * B + q + 1))
                    dve.wait_ge(gu_done, i * 8 + (2 * B + q + 1))
                    dve.wait_ge(alo_done, i * 8 + (2 * B + q - 1))
                    product(q, mix_w[:, span(i * 4 + (q // 4 * 2 + q // 2 % 2), 1)])
                    if not first or q >= 1:
                        dve.wait_ge(ahi_done, i * 8 + (2 * B + q))
                        dve.wait_ge(down_done, i * 8 + (2 * B + q - 4))
                        act_part_lo(q - 1)
                    if first and q in (1, 3):
                        take_shared(B - 2 + q // 2, q // 2, (B - 2 + q // 2) * S)
                    if q == 2:
                        if norming:
                            take_batch(i - 1, 1)
                        if routing:
                            h_lo(i - 2)
                    if q == 3 and routing:
                        choose(i - 2)
                    if q == 4 and norming:
                        statistics(i - 1)
                    if q == 5 and routing:
                        gates(i - 2)
                    if q == 7:
                        take_batch(i, 0)
                        if routing:
                            copy_gates(i - 2)

            dve.wait_ge(pick, 2 * B + 2)
            dve.wait_ge(const_done, 1)
            chosen_turn(0, first=True, norming=False, routing=False)
            chosen_turn(1, routing=False)
            with dve.Fori(2, NB) as i:
                chosen_turn(i)

            def chunk_parts(k, m, early):
                his = act_hi_count(m)
                if not early:
                    dve.wait_ge(y_done, k * CH + (m - 5))
                if act_hi(m % CH):
                    dve.wait_ge(shi_act, k * ACT_HIS + his)
                else:
                    dve.wait_ge(silu_done, k * CH + (m + 1))
                    dve.tensor_copy(s16[:, m % 6, 0, :], s_sb[m % 6]).then_inc(shi_dve, 1)
                    dve.wait_ge(shi_dve, k * DVE_HIS + (m + 1 - his))
                dve.tensor_tensor(s16[:, m % 6, 1, :], s_sb[m % 6], s16[:, m % 6, 0, :],
                                  ALU.subtract).then_inc(slo_done, 1)

            def scale_routed(n, chunks=ROUTED):
                dve.wait_ge(y_done, n * CH + chunks)
                dve.wait_ge(yg_copied, n + 2)
                dve.tensor_tensor(y_gate, ps_yr[:, :], y_gate, ALU.mult).then_inc(yr_taken, 1)

            def add_y(n, cols=slice(0, BT)):
                dve.wait_ge(y_done, n * CH + CH)
                dve.wait_ge(yr_taken, n + 1)
                dve.wait_ge(yT_done, n + 1)
                dve.scalar_tensor_tensor(out=y_sum[:, cols], in0=ps_ys[:, cols], scalar=scales[:, scale_of(0, FC)],
                                         in1=y_gate[:, cols], op0=ALU.mult, op1=ALU.add).then_inc(ysum_done, 1)

            def finish(n):
                dve.wait_ge(yT_done, n + 2)
                dve.wait_ge(out_stored, n * 16 + 16)
                dve.tensor_tensor(out_sb, ps_a[:, :], x_tok[:, span(n * BT, BT)],
                                  ALU.add).then_inc(out_ready, 1)

            def finish_last(half):
                at = half * S
                dve.wait_ge(yT_done, NB + 1 + half)
                dve.wait_ge(out_stored, NB * 16)
                dve.tensor_tensor(out_sb[:, at:at + S], (ps_a, ps_b)[half][:, 0:S],
                                  x_tok[:, (NB - 1) * BT + at:(NB - 1) * BT + at + S],
                                  ALU.add).then_inc(out_ready, 1)

            def ffn_turn(k, first=False, second=False):
                for c in range(CH):
                    if first and c == 0:
                        dve.wait_ge(prod_done, 6 * B)
                        dve.wait_ge(down_done, 6 * B - 4)
                        dve.tensor_copy(a16[:, 3, 0, :], a_sb[:, 1, :]).then_inc(ahi_done, 1)
                        dve.wait_ge(ahi_done, 6 * B)
                        act_part_lo(7)
                    if not first and c == (3 if second else 2):
                        scale_routed(k - 1, CH if second else ROUTED)
                    if not first or c >= 1:
                        chunk_parts(k, c - 1, first and c < 7)
                    if not first and c == 5:
                        add_y(k - 1)
                    for f in DVE_MASKS[not first]:
                        if c == (max(FC * f - 4, 0) if first else 1):
                            if first and f == 1:
                                dve.wait_ge(gu_done, 6 * B)
                                dve.wait_ge(mask_in, 16)
                            if f > HM:
                                dve.wait_ge(z_done, k * CH + (f - HM + first) * FC)
                            elif not first:
                                dve.wait_ge(z_done, mask_use(k, f, second))
                            mask_tokens(dve, k, f).then_inc(hm_dve, 1)
                    if (first and c == 17) or (second and c == 16):
                        copy_gates(k + 2)
                    if not first and c == 12:
                        finish(k - 1)
                    if first:
                        if c == 2:
                            h_lo(2)
                        if c == 3:
                            take_batch(3, 1)
                        if c == 6:
                            choose(2)
                        if c == 8:
                            statistics(3)
                        if c == 13:
                            gates(2)
                    if second:
                        if c == 5:
                            h_lo(3)
                        if c == 7:
                            choose(3)
                        if c == 9:
                            gates(3)

            ffn_turn(0, first=True)
            ffn_turn(1, second=True)
            with dve.Fori(2, NB) as k:
                ffn_turn(k)
            chunk_parts(NB, -1, False)
            scale_routed(NB - 1)
            for half in range(2):
                add_y(NB - 1, slice(half * S, half * S + S))
            for half in range(2):
                finish_last(half)

        @block.gpsimd
        def _(pool):
            pool.memset(ident[:, :], 0.0).then_inc(const_step, 1)
            pool.wait_ge(const_step, 1)
            pool.affine_select(out=ident[:, :], in_=ident[:, :], compare_op=ALU.not_equal, fill=1.0, base=0,
                               pattern=[[-1, P]], channel_multiplier=1).then_inc(const_step, 1)
            pool.wait_ge(const_step, 2)
            for e in range(NE):
                pool.memset(rank_desc[:, :, e], float(NE - e))
            pool.memset(neg_half[:, :], -0.5).then_inc(const_step, 1)
            pool.memset(route[:, :, :], 0.0).then_inc(const_done, 1)

            pool.wait_ge(expert_in[0], 48)
            pool.tensor_scalar(w16[:, w_hi(0, 0, W)], region[:, SLOTS[0] * W:(SLOTS[0] + 1) * W], WS, None,
                               ALU.mult).then_inc(e0_hi, 1)

            def shared_turn(i, first):
                for q in range(4):
                    pool.wait_ge(ahi_done, i * 4 + (q + 1))
                    if not first:
                        pool.wait_ge(down_done, i * 4 + (q - 3))
                    pool.tensor_tensor(a16[:, q, 1, :], a_sb[:, q % 2, :], a16[:, q, 0, :],
                                       ALU.subtract).then_inc(alo_done, 1)

            shared_turn(0, True)
            with pool.Fori(1, B // 2) as i:
                shared_turn(i, False)

            def round_weights(f):
                one, two, all3 = slice(3 * f, 3 * f + FC), scale_of(f, FC), slice(3 * f, 3 * f + 3)
                pool.wait_ge(abs_done, f + 1)
                pool.tensor_scalar(scales[:, one], sums[:, one], 1.0 / D, MIN_SCALE, ALU.mult, ALU.max)
                pool.tensor_scalar(scales[:, two], sums[:, two], 1.0 / F, MIN_SCALE, ALU.mult,
                                   ALU.max).then_inc(tstep, 1)
                pool.wait_ge(tstep, 3 * f + 1)
                for sign in range(2):
                    last = pool.tensor_scalar(halves[:, sign, all3], scales[:, all3], 0.5 - sign, None, ALU.mult)
                last.then_inc(thr_done, 1)
                pool.wait_ge(thr_done, f + 1)
                for sign, (dst, op) in enumerate(((above, ALU.is_gt), (below, ALU.is_lt))):
                    for c in range(FC):
                        n = f * FC + c
                        pool.tensor_scalar(dst[:, c * P:(c + 1) * P], f1_raw[:, n * P:(n + 1) * P],
                                           halves[:, sign, scale_of(f, c)], None, op)
                    last = pool.tensor_scalar(dst[:, F:TW], f2_raw[:, f * F:(f + 1) * F],
                                              halves[:, sign, scale_of(f, FC)], None, op)
                last.then_inc(tstep, 1)
                pool.wait_ge(tstep, 3 * f + 2)
                pool.tensor_tensor(tern[:, f * TW:(f + 1) * TW], above[:, :], below[:, :],
                                   ALU.subtract).then_inc(tern_done, 1)
                pool.wait_ge(tern_done, f + 1)
                pool.sem_inc(tstep, 1)

            def deviation(n):
                pool.wait_ge(stats_done, n + 1)
                pool.tensor_tensor(mean_sum[:, :], stats[:, :, 1], stats[:, :, 4], ALU.add)
                pool.tensor_tensor(mean_dif[:, :], stats[:, :, 1], stats[:, :, 4], ALU.subtract)
                pool.tensor_tensor(sq_sum[:, :], stats[:, :, 2], stats[:, :, 5], ALU.add).then_inc(lstep, 1)
                pool.wait_ge(lstep, 5 * n + 1)
                pool.tensor_tensor(dif_sq[:, :], mean_dif[:, :], mean_dif[:, :], ALU.mult)
                pool.tensor_scalar(neg_mean[:, :], mean_sum[:, :], -0.5, None, ALU.mult)
                pool.tensor_scalar(in_var[:, :], sq_sum[:, :], 1.0 / D, LN_EPS, ALU.mult, ALU.add).then_inc(lstep, 1)
                pool.wait_ge(lstep, 5 * n + 2)
                pool.tensor_scalar(dif_var[:, :], dif_sq[:, :], 0.25, None, ALU.mult).then_inc(lstep, 1)
                pool.wait_ge(lstep, 5 * n + 3)
                pool.tensor_tensor(var_e[:, :], in_var[:, :], dif_var[:, :], ALU.add).then_inc(lstep, 1)
                pool.wait_ge(lstep, 5 * n + 4)
                pool.wait_ge(norm_done, n)
                pool.tensor_tensor(rstd[:, :], var_e[:, :], neg_half[:, :], ALU.pow).then_inc(lstep, 1)
                pool.wait_ge(lstep, 5 * n + 5)
                pool.tensor_tensor(shift[:, :], neg_mean[:, :], rstd[:, :], ALU.mult).then_inc(rstd_done, 1)
                pool.wait_ge(rstd_done, n + 1)

            pool.wait_ge(const_step, 3)
            round_weights(0)
            for f in range(1, NF):
                round_weights(f)
                if f % 2 == 1 and f >= 3:
                    deviation(f // 2 - 1)

            def mask_turn(k, first=False, second=False):
                if first:
                    pool.wait_ge(gu_done, 6 * B)
                pool.wait_ge(mask_in, k * 16 + 16)
                pool.wait_ge(hlo_done, k + 2)
                for f in range(1, NF):
                    if first and f == 7:
                        deviation(NB - 1)
                    if f in DVE_MASKS[not first]:
                        continue
                    if f > HM:
                        pool.wait_ge(z_done, k * CH + (f - HM + first) * FC)
                    elif not first:
                        pool.wait_ge(z_done, mask_use(k, f, second))
                    mask_tokens(pool, k, f).then_inc(hm_pool, 1)

            mask_turn(0, first=True)
            mask_turn(1, second=True)
            with pool.Fori(2, NB) as k:
                mask_turn(k)


_INS = ["x", "cond_8", "L0_cond_skill_gate", "L0_cond_skill_up", "L0_cond_skill_down", "L0_cond_shared_gate",
        "L0_cond_shared_up", "L0_cond_shared_down", "L0_ffn_shared_w1", "L0_ffn_shared_w2", "L0_ffn_expert_w1",
        "L0_ffn_expert_w2", "L0_ffn_router_w", "L0_ffn_ln_gamma", "L0_ffn_ln_beta"]


def kernel(**inputs):
    import numpy as np
    import concourse.bacc as bacc
    from concourse.bass_utils import run_bass_kernel_spmd

    nc = bacc.Bacc("TRN2", target_bir_lowering=False, num_devices=1)
    arrays, args = {}, []
    for name in _INS:
        a = np.ascontiguousarray(inputs[name])
        arrays[f"in_{name}"] = a
        args.append(nc.dram_tensor(f"in_{name}", a.shape, mybir.dt.from_np(a.dtype), kind="ExternalInput").ap())
    out = nc.dram_tensor("out", arrays["in_x"].shape, F32, kind="ExternalOutput").ap()
    moe_adaln_ffn(nc, *args, out)
    r = run_bass_kernel_spmd(nc, [arrays], core_ids=[0])
    return r.results[0]["out"]
```
